# Optimizing a Trainium2 kernel written in Bass

```python
import numpy as np
import jax
import jax.numpy as jnp

def _softmax(x, axis=-1):
    return jax.nn.softmax(x, axis=axis)

def _gelu(x):
    return jax.nn.gelu(x, approximate=True)

def _silu(x):
    return jax.nn.silu(x)

def _sigmoid(x):
    return jax.nn.sigmoid(x)

def _layernorm(x, axis=-1, eps=1e-05):
    m = jnp.mean(x, axis=axis, keepdims=True)
    v = jnp.var(x, axis=axis, keepdims=True)
    return (x - m) / jnp.sqrt(v + eps)

def _scatter_add(tgt, idx, src, axis=0):
    return tgt.at[idx].add(src)

def _segment_sum(src, seg, n):
    return jax.ops.segment_sum(src, seg, n)
kernel_name = 'mk_cond_resid_d2_seqx_r4_adc060'

def setup_inputs(seed: int=0):
    np.random.seed(seed)
    _w = jnp.asarray

    def _rec_inputs():
        import jax
        import jax.numpy as jnp
        _rk = jax.random.key(seed)
        x = 0.0001734 + 0.8201 * jax.random.normal(jax.random.fold_in(_rk, 1), (128, 64, 1024), jnp.float32)
        _lenS = 64 - jax.random.randint(jax.random.fold_in(_rk, 7), (128,), 0, max(1, 64 // 4) + 1, jnp.int32)
        _lenS2 = 64 - jax.random.randint(jax.random.fold_in(_rk, 8), (128,), 0, max(1, 64 // 4) + 1, jnp.int32)
        itok_B_0_7 = jax.random.randint(jax.random.fold_in(_rk, 11), (128,), 0, 8, jnp.int32)
        itok_B_2182_4065 = jax.random.randint(jax.random.fold_in(_rk, 13), (128,), 2182, 4066, jnp.int32)
        itok_B_78_3631 = jax.random.randint(jax.random.fold_in(_rk, 14), (128,), 78, 908, jnp.int32)
        return (x, itok_B_0_7, itok_B_2182_4065, itok_B_78_3631, _lenS)
    x, itok_B_0_7, itok_B_2182_4065, itok_B_78_3631, _lenS = _rec_inputs()

    def _L0_cond_setup():
        import jax, jax.numpy as jnp
        import numpy as np
        SESSION_CHANNELS = [128, 160, 192, 224, 240, 248, 252, 64]
        N_SESS = len(SESSION_CHANNELS)
        B, MAX_C, MAX_T = (16, 64, 1024)
        HID, N_SRC = (128, 64)
        key = jax.random.key(seed)
        ks = jax.random.split(key, 7)
        session_ids = jax.random.randint(ks[0], (B,), 0, N_SESS)
        chan_table = jnp.asarray(SESSION_CHANNELS)
        channel_counts = chan_table[session_ids]
        seq_lens = jax.random.randint(ks[1], (B,), MAX_T // 2, MAX_T + 1)
        x = jax.random.normal(ks[2], (B, MAX_C, MAX_T), jnp.float32)
        cmask = (jnp.arange(MAX_C)[None, :] < channel_counts[:, None]).astype(x.dtype)
        tmask = (jnp.arange(MAX_T)[None, :] < seq_lens[:, None]).astype(x.dtype)
        x = x * cmask[:, :, None] * tmask[:, None, :]
        lim1 = 1.0 / np.sqrt(MAX_C)
        W_sess = jax.random.uniform(ks[3], (N_SESS, MAX_C, HID), jnp.float32, -lim1, lim1)
        b_sess = jax.random.uniform(ks[4], (N_SESS, HID), jnp.float32, -lim1, lim1)
        lim2 = 1.0 / np.sqrt(HID)
        W2 = jax.random.uniform(ks[5], (HID, N_SRC), jnp.float32, -lim2, lim2)
        b2 = jax.random.uniform(ks[6], (N_SRC,), jnp.float32, -lim2, lim2)
        return dict(x=x, session_ids=session_ids, channel_counts=channel_counts, seq_lens=seq_lens, W_sess=W_sess, b_sess=b_sess, W2=W2, b2=b2)
    _L0_cond_all = _L0_cond_setup()
    _L0_cond_in = {k: v for k, v in _L0_cond_all.items() if k in ('W_sess', 'b_sess', 'W2', 'b2')}
    del _L0_cond_all

    def _L1_cond_setup():
        import math
        import jax, jax.numpy as jnp
        import numpy as np
        B, H, N, L = (16, 64, 64, 1024)
        DT_MIN, DT_MAX = (0.001, 0.1)

        def _get_kernel(log_dt, C, log_A_real, A_imag, length):
            dt = jnp.exp(log_dt)
            Cc = C[..., 0] + 1j * C[..., 1]
            A = -jnp.exp(log_A_real) + 1j * A_imag
            dtA = A * dt[:, None]
            Ct = Cc * (jnp.exp(dtA) - 1.0) / A
            P = dtA[:, :, None] * jnp.arange(length, dtype=jnp.float32)
            K = 2.0 * jnp.einsum('hn,hnl->hl', Ct, jnp.exp(P)).real
            return K
        key = jax.random.key(seed)
        ks = jax.random.split(key, 5)
        u = jax.random.normal(ks[0], (B, H, L), dtype=jnp.float32)
        log_dt = jax.random.uniform(ks[1], (H,), dtype=jnp.float32) * (math.log(DT_MAX) - math.log(DT_MIN)) + math.log(DT_MIN)
        C = jax.random.normal(ks[2], (H, N, 2), dtype=jnp.float32)
        log_A_real = jnp.log(0.5 * jnp.ones((H, N), dtype=jnp.float32))
        A_imag = math.pi * jnp.broadcast_to(jnp.arange(N, dtype=jnp.float32), (H, N))
        D = jax.random.normal(ks[3], (H,), dtype=jnp.float32)
        length = jax.random.randint(ks[4], (B,), 1, L + 1, dtype=jnp.int32)
        return {'u': u, 'log_dt': log_dt, 'C': C, 'log_A_real': log_A_real, 'A_imag': A_imag, 'D': D, 'length': length}
    _L1_cond_all = _L1_cond_setup()
    _L1_cond_in = {k: v for k, v in _L1_cond_all.items() if k in ('log_dt', 'C', 'log_A_real', 'A_imag', 'D')}
    del _L1_cond_all
    return {'x': x, 'itok_B_0_7': itok_B_0_7, 'itok_B_2182_4065': itok_B_2182_4065, 'itok_B_78_3631': itok_B_78_3631, '_lenS': _lenS, 'L0_cond_W_sess': _L0_cond_in['W_sess'], 'L0_cond_b_sess': _L0_cond_in['b_sess'], 'L0_cond_W2': _L0_cond_in['W2'], 'L0_cond_b2': _L0_cond_in['b2'], 'L1_cond_log_dt': _L1_cond_in['log_dt'], 'L1_cond_C': _L1_cond_in['C'], 'L1_cond_log_A_real': _L1_cond_in['log_A_real'], 'L1_cond_A_imag': _L1_cond_in['A_imag'], 'L1_cond_D': _L1_cond_in['D']}

def reference(x, itok_B_0_7, itok_B_2182_4065, itok_B_78_3631, _lenS, L0_cond_W_sess, L0_cond_b_sess, L0_cond_W2, L0_cond_b2, L1_cond_log_dt, L1_cond_C, L1_cond_log_A_real, L1_cond_A_imag, L1_cond_D):
    import jax
    import jax.numpy as jnp

    def _L0_cond_ref(x, session_ids, channel_counts, seq_lens, W_sess, b_sess, W2, b2):
        import jax, jax.numpy as jnp
        import numpy as np
        SESSION_CHANNELS = [128, 160, 192, 224, 240, 248, 252, 64]
        N_SESS = len(SESSION_CHANNELS)
        B, MAX_C, MAX_T = (16, 64, 1024)
        HID, N_SRC = (128, 64)
        cmask = (jnp.arange(x.shape[1])[None, :] < channel_counts[:, None]).astype(x.dtype)
        xm = x * cmask[:, :, None]
        W = W_sess[session_ids]
        b = b_sess[session_ids]
        h = jnp.einsum('bct,bch->bht', xm, W) + b[:, :, None]
        h = jax.nn.gelu(h, approximate=False)
        out = jnp.einsum('bht,hs->bst', h, W2) + b2[None, :, None]
        tmask = (jnp.arange(x.shape[2])[None, :] < seq_lens[:, None]).astype(x.dtype)
        return out * tmask[:, None, :]

    def _L1_cond_ref(u, log_dt, C, log_A_real, A_imag, D, length):
        import math
        import jax, jax.numpy as jnp
        import numpy as np
        B, H, N, L = (16, 64, 64, 1024)
        DT_MIN, DT_MAX = (0.001, 0.1)

        def _get_kernel(log_dt, C, log_A_real, A_imag, length):
            dt = jnp.exp(log_dt)
            Cc = C[..., 0] + 1j * C[..., 1]
            A = -jnp.exp(log_A_real) + 1j * A_imag
            dtA = A * dt[:, None]
            Ct = Cc * (jnp.exp(dtA) - 1.0) / A
            P = dtA[:, :, None] * jnp.arange(length, dtype=jnp.float32)
            K = 2.0 * jnp.einsum('hn,hnl->hl', Ct, jnp.exp(P)).real
            return K
        Bq, Hq, Lq = u.shape
        K = _get_kernel(log_dt, C, log_A_real, A_imag, Lq)
        n = 2 * Lq
        kf = jnp.fft.rfft(K, n=n)
        uf = jnp.fft.rfft(u, n=n)
        y = jnp.fft.irfft(uf * kf[None], n=n)[..., :Lq]
        y = y + u * D[:, None]
        mask = (jnp.arange(Lq)[None, :] < length[:, None]).astype(u.dtype)
        return y * mask[:, None, :]
    x = x + _L0_cond_ref(x, itok_B_0_7, _lenS, itok_B_2182_4065, L0_cond_W_sess, L0_cond_b_sess, L0_cond_W2, L0_cond_b2)
    x = x + _L1_cond_ref(x, L1_cond_log_dt, L1_cond_C, L1_cond_log_A_real, L1_cond_A_imag, L1_cond_D, itok_B_78_3631)
    return x

_drawn_inputs = setup_inputs


def setup_inputs(seed=0):
    import zlib

    import numpy as np

    out = dict(_drawn_inputs(seed))
    spreads = {'L1_cond_log_A_real': (-0.6931471824645996, 0.2)}
    factors = {}
    for name, (base, spread) in spreads.items():
        noise = np.random.default_rng([zlib.crc32(name.encode()), seed]).standard_normal(out[name].shape)
        drawn = base * np.exp(spread * noise) if base else spread * noise
        out[name] = jnp.asarray(drawn.astype(out[name].dtype))
    for name, factor in factors.items():
        out[name] = (out[name] * factor).astype(out[name].dtype)
    return out
```

```python
import math
from contextlib import ExitStack

import concourse.bass as bass
from concourse import mybir

ALU = mybir.AluOpType
ACT = mybir.ActivationFunctionType
AX_X = mybir.AxisListType.X
F32 = mybir.dt.float32
F16 = mybir.dt.float16
I32 = mybir.dt.int32

P = 128
SCALE = 256.0
UNSCALE = 1.0 / (SCALE * SCALE)
MAGIC = 12582912.0
TWO_PI_PARTS = (6.28125, 0.0019350051879882812, 3.019916050561934e-07)
LN2_PARTS = (0.693359375, -2.12194440054691e-04)
HALF_PI = math.pi / 2
PI_BELOW = 3.1415925


def build_cond_residual(
    nc: bass.Bass,
    x: bass.AP,
    session_ids: bass.AP,
    seq_lens: bass.AP,
    conv_lens: bass.AP,
    channel_counts: bass.AP,
    W_sess: bass.AP,
    b_sess: bass.AP,
    W2: bass.AP,
    b2: bass.AP,
    log_dt: bass.AP,
    C: bass.AP,
    log_A_real: bass.AP,
    A_imag: bass.AP,
    D: bass.AP,
    out: bass.AP,
):
    B, H, T = x.shape
    S, _, HID = W_sess.shape
    N = A_imag.shape[1]
    assert B == P and HID == P and 2 * H == P and 2 * N == P
    HALF = T // 2
    PAIRS = B // 2
    NB = T // P
    TA = TB = 32
    assert TA * TB == T and HALF == 512
    KROW = T + P

    x1_dram = nc.dram_tensor("x1_scratch", (H, B, T), F32).ap()
    k_scratch = nc.dram_tensor("k_halves", (2, H, KROW), F16)
    k_dram = k_scratch.ap()

    NX = 4
    NS = 2
    NT = 4

    with ExitStack() as ctx:
        def sb(name, shape, dt):
            return ctx.enter_context(nc.sbuf_tensor(name, shape, dt))

        def sem(name):
            return ctx.enter_context(nc.semaphore(name))

        psum = ctx.enter_context(nc.psum_tensor("psum", [P, 8, HALF], F32))

        ident = sb("ident", [P, P], F32)
        iota_t = sb("iota_t", [P, T], F32)
        times_a = sb("times_a", [P, TA], F32)
        times_b = sb("times_b", [P, TB], F32)
        chan_of_part = sb("chan_of_part", [P, 1], F32)
        part_index = sb("part_index", [P, 1], F32)
        sid_i = sb("sid_i", [P, B], I32)
        cnt_i = sb("cnt_i", [P, B], I32)
        seq_i = sb("seq_i", [P, B], I32)
        len_i = sb("len_i", [P, 1], I32)
        sid_f = sb("sid_f", [P, B], F32)
        cnt_f = sb("cnt_f", [P, B], F32)
        seq_f = sb("seq_f", [P, B], F32)
        seq_pair = sb("seq_pair", [P, PAIRS], F32)
        len_f = sb("len_f", [P, 1], F32)
        live = sb("live", [P, B], F32)
        w_offset_f = sb("w_offset_f", [1, B], F32)
        w_offset = sb("w_offset", [1, B], I32)
        channel_scale = sb("channel_scale", [P, PAIRS], F32)
        scale_now = sb("scale_now", [P, NX], F32)
        onehot = sb("onehot", [S, B], F32)
        bs_sb = sb("bs_sb", [S, HID], F32)
        bias_all = sb("bias_all", [P, B], F32)
        w2_sb = sb("w2_sb", [P, H], F32)
        b2_col = sb("b2_col", [P, 1], F32)
        seq_min = sb("seq_min", [1, 2], F32)
        seq_min_i = sb("seq_min_i", [1, 1], I32)
        ws_raw = sb("ws_raw", [P, S, HID], F32)
        w_tab = sb("w_tab", [P, S, 2, HID], F16)
        zeros16 = sb("zeros16", [H, P], F16)

        par = sb("par", [H, 4 * N], F32)
        par2 = sb("par2", [H, 4, 2, N], F32)
        parT = sb("parT", [P, 4, H], F32)
        ex = sb("ex", [P, 2, H], F32)
        small = sb("small", [P, 28, H], F32)
        expo = sb("expo", [P, 4, H], F32)
        tab_im = sb("tab_im", [P, H, TA], F32)
        tab_k = sb("tab_k", [P, H, TA], F32)
        tab_re = sb("tab_re", [P, H, TA], F32)
        tab_c = sb("tab_c", [P, H, TA], F32)
        gmat = sb("gmat", [P, H, TA], F32)
        emat = sb("emat", [P, H, TB], F32)
        k_hi = sb("k_hi", [TA, H, TB], F16)
        k_lo = sb("k_lo", [TA, H, TB], F16)
        d_row = sb("d_row", [1, H], F32)
        last_a = sb("last_a", [1, TA], F32)
        d_last = sb("d_last", [1, H, TB], F32)

        xt = sb("xt", [P, NX, T], F32)
        xs = sb("xs", [P, NS, 2, T], F16)
        hid = sb("hid", [P, 2, 2, HALF], F32)
        tmp = sb("tmp", [P, HALF], F32)

        toep = sb("toep", [P, NT, 2, T], F16)
        u_hi = sb("u_hi", [P, 2, NB, P], F16)
        u_lo = sb("u_lo", [P, 2, NB, P], F16)
        ys = sb("ys", [P, 2, T], F32)

        s_ids = sem("s_ids")
        s_par = sem("s_par")
        s_wraw = sem("s_wraw")
        s_small = sem("s_small")
        s_iota = sem("s_iota")
        s_ident0 = sem("s_ident0")
        s_ident = sem("s_ident")
        s_chain = sem("s_chain")
        s_onehot = sem("s_onehot")
        s_biasmm = sem("s_biasmm")
        s_bias = sem("s_bias")
        s_zeros = sem("s_zeros")
        s_offset = sem("s_offset")
        s_scale = sem("s_scale")
        s_wsplit = sem("s_wsplit")
        s_par2 = sem("s_par2")
        s_parT = sem("s_parT")
        s_dlast = sem("s_dlast")
        s_parC = sem("s_parC")
        s_ang = sem("s_ang")
        s_trig = sem("s_trig")
        s_gmat = sem("s_gmat")
        s_kmm = sem("s_kmm")
        s_ksplit = sem("s_ksplit")
        s_kstored = sem("s_kstored")

        x_loaded = [sem(f"x_loaded{n}") for n in range(NX)]
        x1_stored = [sem(f"x1_stored{n}") for n in range(NX)]
        scale_copied = sem("scale_copied")
        x_hi_done = sem("x_hi_done")
        x_split = sem("x_split")
        h_ready = sem("h_ready")
        gelu_done = sem("gelu_done")
        o_ready = sem("o_ready")
        x1_ready = sem("x1_ready")
        t_loaded = [sem(f"t_loaded{n}") for n in range(NT)]
        c_loaded = [sem(f"c_loaded{n}") for n in range(NX)]
        out_stored = [sem(f"out_stored{n}") for n in range(NX)]
        turned = sem("turned")
        u_hi_done = sem("u_hi_done")
        u_split = sem("u_split")
        conv_done = sem("conv_done")
        y_scaled = sem("y_scaled")
        out_ready = sem("out_ready")
        mask_ready = sem("mask_ready")
        act_passed = sem("act_passed")
        pool_passed = sem("pool_passed")
        dve_passed = sem("dve_passed")
        tmp_done = sem("tmp_done")

        def hid_bank(q, j):
            return psum[:, 2 * q + j, :]

        def mlp_bank(q):
            return psum[:, 4 + q, :]

        def turn_bank(q):
            return psum[:, q, :]

        def y_banks(h):
            return psum[:, 2 + 2 * (h % 2):4 + 2 * (h % 2), :].rearrange("p a n -> p (a n)")

        mask = psum[:, 6:8, :].rearrange("p a n -> p (a n)")

        small_col = {}

        def sm(name):
            if name not in small_col:
                small_col[name] = len(small_col)
            return small[:, small_col[name], :]

        kpsum = psum[0:TA, 0:4, :].rearrange("p a n -> p (a n)").rearrange("p (h b) -> p h b", b=TB)


        STEPS = PAIRS // NX
        CSTEPS = H // NX

        block = ctx.enter_context(nc.Block())

        @block.sync
        def _(sp):
            for ap, src in ((sid_i, session_ids), (cnt_i, channel_counts), (seq_i, seq_lens)):
                sp.dma_start(ap[:], src.partition_broadcast(P)).then_inc(s_ids, 16)
            sp.dma_start(len_i[:], conv_lens.rearrange("(b a) -> b a", a=1)).then_inc(s_ids, 16)
            for j in range(2):
                sp.dma_start(ws_raw[j * H:(j + 1) * H, :, :], W_sess.rearrange("s c d -> c s d")).then_inc(s_wraw, 16)
            sp.dma_start(bs_sb[:], b_sess).then_inc(s_small, 16)
            sp.dma_start(w2_sb[:], W2).then_inc(s_small, 16)
            for j in range(2):
                sp.dma_start(b2_col[j * H:(j + 1) * H, :], b2.rearrange("(s a) -> s a", a=1)).then_inc(s_small, 16)
            sp.dma_start(d_row[:], D.rearrange("(a h) -> a h", a=1)).then_inc(s_small, 16)
            sp.dma_start(ex[:, 0, :], log_dt.partition_broadcast(P)).then_inc(s_par, 16)
            sp.dma_start(par[:, 0:N], log_A_real).then_inc(s_par, 16)
            sp.dma_start(par[:, N:2 * N], A_imag).then_inc(s_par, 16)
            sp.dma_start(par[:, 2 * N:4 * N], C.rearrange("h n z -> h (n z)")).then_inc(s_par, 16)

            def load_x(p, slot):
                sp.dma_start(xt[:, slot, :], x[bass.ds(2 * p, 2)].rearrange("b c t -> (b c) t")).then_inc(x_loaded[slot], 16)

            def store_x1(p, slot):
                for j in range(2):
                    sp.dma_start(x1_dram[:, bass.ds(2 * p + j, 1), :].rearrange("c b t -> (c b) t"),
                                 xt[j * H:(j + 1) * H, slot, :]).then_inc(x1_stored[slot], 16)

            def stage1_step(i, first, last):
                for s in range(NX):
                    p = i * NX + s
                    sp.wait_ge(x1_ready, 2 * p + 2)
                    store_x1(p, s)
                    if not (last and s > 0):
                        nxt = (s + NX - 1) % NX
                        if not (first and s == 0):
                            sp.wait_ge(x1_stored[nxt], 32 * (i + (1 if s > 0 else 0)))
                            load_x(p + NX - 1, nxt)

            for s in range(NX):
                load_x(s, s)
            sp.wait_ge(s_zeros, 1)
            sp.wait_ge(s_ksplit, 2)
            for half, src in enumerate((k_hi, k_lo)):
                sp.dma_start(k_dram[half, :, 0:T].rearrange("h (a b) -> a h b", b=TB), src[:]).then_inc(s_kstored, 16)
                sp.dma_start(k_dram[half, :, T:KROW], zeros16[:]).then_inc(s_kstored, 16)

            stage1_step(0, True, False)
            with sp.Fori(1, STEPS - 1) as i:
                stage1_step(i, False, False)
            stage1_step(STEPS - 1, False, True)

            def load_toeplitz(h, slot):
                row = k_dram[:, bass.ds(h, 1), :]
                sp.dma_start(toep[:, slot, :, :], bass.AP(k_scratch, row.offset, [[1, P], [H * KROW, 2], [1, T]])
                             ).then_inc(t_loaded[slot], 16)

            def load_channel(h, slot):
                sp.dma_start(xt[:, slot, :], x1_dram[bass.ds(h, 1)].rearrange("a b t -> (a b) t")).then_inc(c_loaded[slot], 16)

            def store_out(h, slot):
                sp.dma_start(out[:, bass.ds(h, 1), :].rearrange("b a t -> (b a) t"), xt[:, slot, :]).then_inc(out_stored[slot], 16)

            def stage2_step(i, first, last):
                for s in range(NX):
                    h = i * NX + s
                    sp.wait_ge(out_ready, h + 1)
                    store_out(h, s)
                    if not (last and s > 0) and not (first and s == 0):
                        nxt = (s + NX - 1) % NX
                        sp.wait_ge(out_stored[nxt], 16 * (i + (1 if s > 0 else 0)))
                        load_channel(h + NX - 1, nxt)
                        load_toeplitz(h + NX - 1, nxt)

            sp.wait_ge(s_kstored, 64)
            for s in range(NX):
                load_toeplitz(s, s)
            for s in range(NX):
                sp.wait_ge(x1_stored[s], 32 * STEPS)
            for s in range(NX):
                load_channel(s, s)
            stage2_step(0, True, False)
            with sp.Fori(1, CSTEPS - 1) as i:
                stage2_step(i, False, False)
            stage2_step(CSTEPS - 1, False, True)
            for s in range(NX):
                sp.wait_ge(out_stored[s], 16 * CSTEPS)

        @block.gpsimd
        def _(pool):
            nc.gpsimd.iota(iota_t[:], pattern=[[1, T]], base=0, channel_multiplier=0,
                           allow_small_or_imprecise_dtypes=True).then_inc(s_iota, 1)
            nc.gpsimd.iota(times_a[:], pattern=[[-TB, TA]], base=T - TB, channel_multiplier=0,
                           allow_small_or_imprecise_dtypes=True).then_inc(s_iota, 1)
            nc.gpsimd.iota(times_b[:], pattern=[[-1, TB]], base=TB - 1, channel_multiplier=0,
                           allow_small_or_imprecise_dtypes=True).then_inc(s_iota, 1)
            nc.gpsimd.iota(part_index[:], pattern=[[0, 1]], base=0, channel_multiplier=1,
                           allow_small_or_imprecise_dtypes=True).then_inc(s_iota, 1)
            nc.gpsimd.memset(ident[:], 0.0).then_inc(s_ident0, 1)
            pool.wait_ge(s_ident0, 1)
            nc.gpsimd.affine_select(out=ident[:], in_=ident[:], compare_op=ALU.not_equal, fill=1.0, base=0,
                                    pattern=[[-1, P]], channel_multiplier=1).then_inc(s_ident, 1)

            def copy_scales(i):
                nc.gpsimd.tensor_copy(scale_now[:], channel_scale[:, bass.ds(i * NX, NX)]).then_inc(scale_copied, 1)

            def split_hi(i, s, first):
                p = i * NX + s
                pool.wait_ge(x_loaded[s], 16 * (i + 1))
                if not (first and s < NS):
                    pool.wait_ge(h_ready, 2 * (p - NS) + 2)
                if s == 0:
                    pool.wait_ge(scale_copied, i + 1)
                pool.sem_inc(pool_passed, 1)
                for j in range(2):
                    q = slice(j * H, (j + 1) * H)
                    nc.gpsimd.tensor_scalar(xs[q, s % NS, j, :], xt[q, s, :], scale_now[q, s:s + 1], None,
                                            ALU.mult).then_inc(x_hi_done, 1)

            def step(i, first):
                if not first:
                    pool.wait_ge(x_hi_done, 2 * NX * i)
                copy_scales(i)
                for s in range(NX):
                    split_hi(i, s, first)

            pool.wait_ge(s_scale, 1)
            step(0, True)
            with pool.Fori(1, STEPS) as i:
                step(i, False)

        @block.scalar
        def _(act):
            act.wait_ge(s_ang, 1)
            nc.scalar.activation(sm("t_step"), sm("t_step_arg"), ACT.Tanh).then_inc(s_trig, 1)
            nc.scalar.activation(sm("sin_half"), sm("half_arg"), ACT.Sin).then_inc(s_trig, 1)
            nc.scalar.activation(sm("cos_half"), sm("half_arg_c"), ACT.Sin).then_inc(s_trig, 1)
            act.wait_ge(s_ang, 2)
            nc.scalar.activation(tab_re[:], tab_re[:], ACT.Tanh, scale=0.5).then_inc(s_trig, 1)
            nc.scalar.activation(tab_c[:], tab_c[:], ACT.Sin).then_inc(s_trig, 1)
            nc.scalar.activation(tab_im[:], tab_im[:], ACT.Sin).then_inc(s_trig, 1)
            act.wait_ge(s_ang, 3)
            nc.scalar.activation(tab_re[:], tab_re[:], ACT.Tanh, scale=0.5).then_inc(s_trig, 1)
            nc.scalar.activation(tab_im[:], tab_im[:], ACT.Sin).then_inc(s_trig, 1)

            act.wait_ge(s_bias, 1)

            def step(i, first, last):
                for s in range(NX):
                    for q in range(2):
                        u = i * 2 * NX + 2 * s + q
                        uu = 2 * s + q
                        act.wait_ge(h_ready, u + 1)
                        if not (first and uu < 2):
                            act.wait_ge(o_ready, u - 1)
                        act.sem_inc(act_passed, 1)
                        for j in range(2):
                            nc.scalar.activation(hid[:, q, j, :], hid_bank(q, j), ACT.Gelu,
                                                 bias=bias_all[:, bass.ds(i * 2 * NX + 2 * s + j, 1)],
                                                 scale=UNSCALE).then_inc(gelu_done, 1)

            step(0, True, False)
            with act.Fori(1, STEPS) as i:
                step(i, False, False)

            def split_hi(i, s, first):
                h = i * NX + s
                for q in range(2):
                    act.wait_ge(turned, 2 * h + q + 1)
                    if q == 0 and not (first and s < 2):
                        act.wait_ge(conv_done, h - 1)
                    nc.scalar.activation(u_hi[:, s % 2, q * (NB // 2):(q + 1) * (NB // 2), :].rearrange("p k b -> p (k b)"),
                                         turn_bank(q), ACT.Copy, scale=SCALE).then_inc(u_hi_done, 1)

            def unscale(h, s, first):
                act.wait_ge(conv_done, h + 1)
                if not (first and s < 2):
                    act.wait_ge(out_ready, h - 1)
                y = y_banks(s)
                nc.scalar.activation(ys[:, s % 2, :], bass.AP(y.tensor, y.offset + T - 1, [y.ap[0], [-1, T]]), ACT.Copy, scale=UNSCALE).then_inc(y_scaled, 1)

            def step2(i, first, last):
                for s in range(NX):
                    if s < NX - 1:
                        split_hi(i, s + 1, first)
                    elif not last:
                        split_hi(i + 1, 0, False)
                    unscale(i * NX + s, s, first)

            split_hi(0, 0, True)
            step2(0, True, False)
            with act.Fori(1, CSTEPS - 1) as i:
                step2(i, False, False)
            step2(CSTEPS - 1, False, True)

        @block.vector
        def _(dve):
            chain = [0]

            def link(ins):
                chain[0] += 1
                ins.then_inc(s_chain, 1)
                dve.wait_ge(s_chain, chain[0])

            V = nc.vector
            V.memset(zeros16[:], 0.0).then_inc(s_zeros, 1)

            dve.wait_ge(s_par, 64)
            c_parts = par[:, 2 * N:4 * N].rearrange("h (n z) -> h n z", z=2)
            for k, v in enumerate((par[:, 0:N], par[:, N:2 * N], c_parts[:, :, 0], c_parts[:, :, 1])):
                ins = V.tensor_copy(par2[:, k], v.unsqueeze(1).to_broadcast([H, 2, N]))
            ins.then_inc(s_par2, 1)

            dve.wait_ge(s_ids, 64)
            dve.wait_ge(s_iota, 4)
            V.tensor_copy(chan_of_part[0:H, :], part_index[0:H, :])
            V.tensor_scalar(chan_of_part[H:P, :], part_index[H:P, :], float(-H), None, ALU.add)
            V.tensor_copy(sid_f[:], sid_i[:])
            V.tensor_copy(cnt_f[:], cnt_i[:])
            V.tensor_copy(len_f[:], len_i[:])
            link(V.tensor_copy(seq_f[:], seq_i[:]))
            for j in range(2):
                q = slice(j * H, (j + 1) * H)
                V.tensor_copy(seq_pair[q, :], seq_f[q, :].rearrange("p (n j) -> p n j", j=2)[:, :, j])
            link(V.tensor_reduce(seq_min[:, 0:1], seq_f[0:1, :], AX_X, ALU.min))
            link(V.tensor_copy(seq_min_i[:], seq_min[:, 0:1]))
            V.tensor_scalar(onehot[:], sid_f[0:S, :], part_index[0:S, 0:1], None, ALU.is_equal).then_inc(s_onehot, 1)
            V.tensor_scalar(w_offset_f[:], sid_f[0:1, :], float(S - 1), 0.0, ALU.min, ALU.max)
            link(V.tensor_scalar(live[:], cnt_f[:], chan_of_part[:, 0:1], SCALE, ALU.is_gt, ALU.mult))
            V.tensor_scalar(w_offset[:], w_offset_f[:], 2.0 * HID, None, ALU.mult).then_inc(s_offset, 1)
            for j in range(2):
                q = slice(j * H, (j + 1) * H)
                ins = V.tensor_copy(channel_scale[q, :], live[q, :].rearrange("p (n j) -> p n j", j=2)[:, :, j])
            ins.then_inc(s_scale, 1)
            dve.wait_ge(s_wraw, 32)
            link(V.tensor_scalar(w_tab[:, :, 0, :], ws_raw[:], SCALE, None, ALU.mult))
            V.scalar_tensor_tensor(out=w_tab[:, :, 1, :], in0=ws_raw[:], scalar=SCALE, in1=w_tab[:, :, 0, :],
                                   op0=ALU.mult, op1=ALU.subtract).then_inc(s_wsplit, 1)
            dve.wait_ge(s_biasmm, 1)
            V.tensor_copy(bias_all[:], psum[:, 7, 0:B]).then_inc(s_bias, 1)

            dve.wait_ge(s_small, 80)
            V.memset(last_a[:], 0.0)
            link(V.memset(d_last[:], 0.0))
            V.memset(last_a[:, TA - 1:TA], 1.0)
            V.tensor_scalar(d_last[:, :, TB - 1], d_row[:], 1.0, None, ALU.add).then_inc(s_dlast, 1)

            dve.wait_ge(s_parT, 1)
            V.tensor_copy(parT[:], psum[:, 6, 0:4 * H].rearrange("p (k h) -> p k h", k=4)).then_inc(s_parC, 1)
            dve.wait_ge(s_parC, 1)
            dve.wait_ge(s_par, 64)
            link(V.tensor_copy(ex[:, 1, :], parT[:, 0, :]))
            v = ex[:]
            k = expo[:, 0:2, :]
            acc = expo[:, 2:4, :]
            link(V.tensor_scalar(k, v, 1.0 / math.log(2.0), MAGIC, ALU.mult, ALU.add))
            link(V.tensor_scalar(k, k, -MAGIC, None, ALU.add))
            for part in LN2_PARTS:
                link(V.scalar_tensor_tensor(out=v, in0=k, scalar=-part, in1=v, op0=ALU.mult, op1=ALU.add))
            link(V.tensor_scalar(acc, v, 1.0 / math.factorial(7), 1.0 / math.factorial(6), ALU.mult, ALU.add))
            for n in range(5, -1, -1):
                link(V.tensor_tensor(acc, acc, v, ALU.mult))
                link(V.tensor_scalar(acc, acc, 1.0 / math.factorial(n), None, ALU.add))
            link(V.tensor_scalar(v.bitcast(I32), k, 127.0, float(1 << 23), ALU.add, ALU.mult))
            link(V.tensor_tensor(ex[:], acc, v, ALU.mult))
            dt, rate = ex[:, 0, :], ex[:, 1, :]
            a_im, c_re, c_im = parT[:, 1, :], parT[:, 2, :], parT[:, 3, :]
            V.tensor_tensor(sm("im"), a_im, dt, ALU.mult)
            V.tensor_scalar(sm("a_re"), rate, -1.0, None, ALU.mult)
            link(V.tensor_tensor(sm("re0"), rate, dt, ALU.mult))
            link(V.tensor_scalar(sm("re"), sm("re0"), -1.0, None, ALU.mult))

            def reduce_angle(ang, k):
                link(V.tensor_scalar(k, ang, 1.0 / (2.0 * math.pi), MAGIC, ALU.mult, ALU.add))
                link(V.tensor_scalar(k, k, -MAGIC, None, ALU.add))
                for part in TWO_PI_PARTS:
                    link(V.scalar_tensor_tensor(out=ang, in0=k, scalar=-part, in1=ang, op0=ALU.mult, op1=ALU.add))
                link(V.tensor_scalar(ang, ang, PI_BELOW, -PI_BELOW, ALU.min, ALU.max))

            def cosine_argument(dst, ang):
                link(V.scalar_tensor_tensor(out=dst, in0=ang, scalar=-1.0, in1=ang, op0=ALU.mult, op1=ALU.min))
                return V.tensor_scalar(dst, dst, HALF_PI, None, ALU.add)

            link(V.tensor_copy(sm("step"), sm("im")))
            reduce_angle(sm("step"), sm("k1"))
            link(V.tensor_scalar(sm("half_arg"), sm("step"), 0.5, None, ALU.mult))
            link(cosine_argument(sm("half_arg_c"), sm("half_arg")))
            V.tensor_scalar(sm("t_step_arg"), sm("re"), 0.5, None, ALU.mult).then_inc(s_ang, 1)

            def tab(ap, n, steps):
                return (ap.unsqueeze(2).to_broadcast([P, H, n]), steps.unsqueeze(1).to_broadcast([P, H, n]))

            V.tensor_tensor(tab_im[:], *tab(sm("im"), TA, times_a[:]), ALU.mult)
            link(V.tensor_tensor(tab_re[:], *tab(sm("re"), TA, times_a[:]), ALU.mult))
            reduce_angle(tab_im[:], tab_k[:])
            cosine_argument(tab_c[:], tab_im[:]).then_inc(s_ang, 1)

            dve.wait_ge(s_trig, 3)
            V.tensor_scalar(sm("one_minus_t"), sm("t_step"), -1.0, 1.0, ALU.mult, ALU.add)
            V.tensor_tensor(sm("sin2"), sm("sin_half"), sm("sin_half"), ALU.mult)
            V.tensor_tensor(sm("sincos"), sm("sin_half"), sm("cos_half"), ALU.mult)
            V.tensor_tensor(sm("abs2"), sm("a_re"), sm("a_re"), ALU.mult)
            link(V.tensor_tensor(sm("aim2"), a_im, a_im, ALU.mult))
            V.reciprocal(sm("k1"), sm("one_minus_t"))
            link(V.tensor_tensor(sm("abs2"), sm("abs2"), sm("aim2"), ALU.add))
            V.tensor_tensor(sm("em1"), sm("k1"), sm("t_step"), ALU.mult)
            V.tensor_scalar(sm("aim2"), sm("sin2"), -2.0, 1.0, ALU.mult, ALU.add)
            link(V.reciprocal(sm("inv"), sm("abs2")))
            V.tensor_scalar(sm("k1"), sm("em1"), 2.0, 1.0, ALU.mult, ALU.add)
            link(V.tensor_tensor(sm("er"), sm("em1"), sm("aim2"), ALU.mult))
            V.tensor_tensor(sm("er"), sm("er"), sm("sin2"), ALU.subtract)
            link(V.tensor_tensor(sm("ei"), sm("k1"), sm("sincos"), ALU.mult))
            V.tensor_tensor(sm("zr"), sm("er"), sm("a_re"), ALU.mult)
            V.tensor_tensor(sm("k1"), sm("ei"), a_im, ALU.mult)
            V.tensor_tensor(sm("zi"), sm("ei"), sm("a_re"), ALU.mult)
            link(V.tensor_tensor(sm("sin2"), sm("er"), a_im, ALU.mult))
            V.tensor_tensor(sm("zr"), sm("zr"), sm("k1"), ALU.add)
            V.tensor_tensor(sm("zi"), sm("zi"), sm("sin2"), ALU.subtract)
            link(V.tensor_scalar(sm("inv"), sm("inv"), 4.0, None, ALU.mult))
            V.tensor_tensor(sm("zr"), sm("zr"), sm("inv"), ALU.mult)
            link(V.tensor_tensor(sm("zi"), sm("zi"), sm("inv"), ALU.mult))
            V.tensor_tensor(sm("k1"), c_re, sm("zr"), ALU.mult)
            V.tensor_tensor(sm("er"), c_im, sm("zi"), ALU.mult)
            V.tensor_tensor(sm("ei"), c_re, sm("zi"), ALU.mult)
            link(V.tensor_tensor(sm("sin2"), c_im, sm("zr"), ALU.mult))
            V.tensor_tensor(sm("er"), sm("k1"), sm("er"), ALU.subtract)
            link(V.tensor_tensor(sm("ei"), sm("ei"), sm("sin2"), ALU.add))
            lo, hi = slice(0, N), slice(N, P)
            V.tensor_copy(sm("gp")[lo], sm("er")[lo])
            V.tensor_scalar(sm("gp")[hi], sm("ei")[hi], -1.0, None, ALU.mult)
            V.tensor_scalar(sm("gq")[lo], sm("ei")[lo], -1.0, None, ALU.mult)
            link(V.tensor_scalar(sm("gq")[hi], sm("er")[hi], -1.0, None, ALU.mult))

            def decay(ap):
                link(V.tensor_scalar(ap, ap, -1.0, 1.0, ALU.mult, ALU.add))
                link(V.reciprocal(ap, ap))
                link(V.tensor_scalar(ap, ap, 2.0, -1.0, ALU.mult, ALU.add))

            dve.wait_ge(s_trig, 6)
            decay(tab_re[:])
            V.tensor_tensor(tab_c[:], tab_c[:], tab_re[:], ALU.mult)
            link(V.tensor_tensor(tab_im[:], tab_im[:], tab_re[:], ALU.mult))
            V.tensor_tensor(tab_c[:], tab_c[:], sm("gp").unsqueeze(2).to_broadcast([P, H, TA]), ALU.mult)
            link(V.tensor_tensor(tab_im[:], tab_im[:], sm("gq").unsqueeze(2).to_broadcast([P, H, TA]), ALU.mult))
            link(V.tensor_tensor(gmat[:], tab_c[:], tab_im[:], ALU.add))
            V.tensor_tensor(tab_im[:], *tab(sm("im"), TB, times_b[:]), ALU.mult)
            link(V.tensor_tensor(tab_re[:], *tab(sm("re"), TB, times_b[:]), ALU.mult))
            reduce_angle(tab_im[:], tab_k[:])
            cosine_argument(tab_im[lo], tab_im[lo]).then_inc(s_ang, 1)
            dve.wait_ge(s_trig, 8)
            decay(tab_re[:])
            V.tensor_tensor(emat[:], tab_im[:], tab_re[:], ALU.mult).then_inc(s_gmat, 1)
            dve.wait_ge(s_kmm, 1)
            V.tensor_scalar(k_hi[:], kpsum, SCALE, None, ALU.mult).then_inc(s_ksplit, 1)
            dve.wait_ge(s_ksplit, 1)
            V.scalar_tensor_tensor(out=k_lo[:].rearrange("p h b -> p (h b)"), in0=kpsum.rearrange("p h b -> p (h b)"),
                                   scalar=SCALE, in1=k_hi[:].rearrange("p h b -> p (h b)"),
                                   op0=ALU.mult, op1=ALU.subtract).then_inc(s_ksplit, 1)

            def split_lo(p, i, s, first):
                for j in range(2):
                    q = slice(j * H, (j + 1) * H)
                    other = slice((1 - j) * H, (2 - j) * H)
                    dve.wait_ge(x_hi_done, 2 * p + j + 1)
                    V.scalar_tensor_tensor(out=xs[other, s % NS, j, :], in0=xt[q, s, :],
                                           scalar=channel_scale[q, bass.ds(p, 1)],
                                           in1=xs[q, s % NS, j, :], op0=ALU.mult, op1=ALU.subtract).then_inc(x_split, 1)

            def add_mlp(i, s, q, masked):
                u = i * 2 * NX + 2 * s + q
                cols = slice(q * HALF, (q + 1) * HALF)
                dve.wait_ge(o_ready, u + 1)
                if not masked:
                    V.scalar_tensor_tensor(out=xt[:, s, cols], in0=mlp_bank(q), scalar=b2_col[:, 0:1],
                                           in1=xt[:, s, cols], op0=ALU.add, op1=ALU.add).then_inc(x1_ready, 1)
                    return
                V.tensor_scalar(tmp[:], mlp_bank(q), b2_col[:, 0:1], None, ALU.add).then_inc(tmp_done, 1)
                dve.wait_ge(tmp_done, 2 * u + 1)
                V.scalar_tensor_tensor(out=tmp[:], in0=iota_t[:, cols], scalar=seq_pair[:, bass.ds(i * NX + s, 1)],
                                       in1=tmp[:], op0=ALU.is_lt, op1=ALU.mult).then_inc(tmp_done, 1)
                dve.wait_ge(tmp_done, 2 * u + 2)
                V.tensor_tensor(xt[:, s, cols], xt[:, s, cols], tmp[:], ALU.add).then_inc(x1_ready, 1)

            def step(i, first, last, masked):
                for s in range(NX):
                    if s < NX - 1:
                        split_lo(i * NX + s + 1, i, s + 1, first)
                    elif not last:
                        split_lo((i + 1) * NX, i + 1, 0, False)
                    for q in range(2):
                        add_mlp(i, s, q, masked)

            def stage1(masked):
                split_lo(0, 0, 0, True)
                step(0, True, False, masked)
                with dve.Fori(1, STEPS - 1) as i:
                    step(i, False, False, masked)
                step(STEPS - 1, False, True, masked)

            shortest = dve.value_load(seq_min_i[0:1, 0:1])
            with dve.If(shortest < T):
                stage1(True)
            with dve.Else():
                stage1(False)

            V.tensor_scalar(mask, iota_t[:], len_f[:, 0:1], None, ALU.is_lt).then_inc(mask_ready, 1)
            dve.wait_ge(mask_ready, 1)

            def split_u(i, s):
                h = i * NX + s
                for q in range(2):
                    blocks = slice(q * (NB // 2), (q + 1) * (NB // 2))
                    dve.wait_ge(u_hi_done, 2 * h + q + 1)
                    V.scalar_tensor_tensor(out=u_lo[:, s % 2, blocks, :].rearrange("p k b -> p (k b)"),
                                           in0=turn_bank(q), scalar=SCALE,
                                           in1=u_hi[:, s % 2, blocks, :].rearrange("p k b -> p (k b)"),
                                           op0=ALU.mult, op1=ALU.subtract).then_inc(u_split, 1)

            def finish(h, s):
                dve.wait_ge(y_scaled, h + 1)
                dve.sem_inc(dve_passed, 1)
                V.copy_predicated(xt[:, s, :], mask.bitcast(I32), ys[:, s % 2, :]).then_inc(out_ready, 1)

            def step2(i, last):
                for s in range(NX):
                    if s < NX - 1:
                        split_u(i, s + 1)
                    elif not last:
                        split_u(i + 1, 0)
                    finish(i * NX + s, s)

            split_u(0, 0)
            with dve.Fori(0, CSTEPS - 1) as i:
                step2(i, False)
            step2(CSTEPS - 1, True)

        @block.tensor
        def _(pe):
            M = nc.tensor.matmul
            pe.wait_ge(s_small, 80)
            pe.wait_ge(s_onehot, 1)
            M(psum[:, 7, 0:B], bs_sb[:], onehot[:], start=True, stop=True).then_inc(s_biasmm, 1)
            pe.wait_ge(s_par2, 1)
            pe.wait_ge(s_ident, 1)
            for k in range(4):
                ins = nc.tensor.transpose(psum[:, 6, k * H:(k + 1) * H], par2[:, k].rearrange("h a n -> h (a n)"),
                                          ident[0:H, 0:H])
            ins.then_inc(s_parT, 1)
            pe.wait_ge(s_dlast, 1)
            pe.wait_ge(s_gmat, 1)
            per_bank = HALF // TB
            for h in range(H):
                if h % per_bank == 0:
                    M(kpsum[:, h:h + per_bank, :], last_a[:], d_last[:, h:h + per_bank, :], start=True, stop=True)
                ins = M(kpsum[:, h, :], gmat[:, h, :], emat[:, h, :], start=False, stop=True,
                        skip_group_check=True)
            ins.then_inc(s_kmm, 1)
            pe.wait_ge(s_ksplit, 2)

            w_flat = w_tab[:].rearrange("p s h d -> p (s h d)")

            def offsets(i):
                _, values = nc.values_load_multi_w_load_instructions(
                    w_offset[0:1, bass.ds(i * 2 * NX, 2 * NX)], engines=[mybir.EngineType.PE],
                    min_val=0, max_val=(S - 1) * 2 * HID,
                    skip_runtime_bounds_check_because="w_offset is clamped to the table where it is made")
                return values

            def hidden(i, s, q, first, at):
                u = i * 2 * NX + 2 * s + q
                if q == 0:
                    pe.wait_ge(x_split, 2 * (i * NX + s) + 2)
                if not (first and s == 0):
                    pe.wait_ge(gelu_done, 2 * (u - 2) + 2)
                for j in range(2):
                    for half in range(2):
                        ins = M(hid_bank(q, j), w_flat[:, bass.ds(at[2 * s + j] + half * HID, HID)],
                                xs[:, s % NS, j, q * HALF:(q + 1) * HALF], start=(half == 0), stop=(half == 1))
                ins.then_inc(h_ready, 1)

            def output(u, q, first):
                pe.wait_ge(gelu_done, 2 * u + 2)
                if not first:
                    pe.wait_ge(x1_ready, u - 1)
                for j in range(2):
                    ins = M(mlp_bank(q)[j * H:(j + 1) * H, :], w2_sb[:], hid[:, q, j, :], start=True, stop=True)
                ins.then_inc(o_ready, 1)

            def step(i, first):
                at = offsets(i)
                for s in range(NX):
                    for q in range(2):
                        uu = 2 * s + q
                        hidden(i, s, q, first, at)
                        if not (first and uu == 0):
                            output(i * 2 * NX + uu - 1, 1 - q, first and uu < 3)

            pe.wait_ge(s_offset, 1)
            pe.wait_ge(s_wsplit, 1)
            step(0, True)
            with pe.Fori(1, STEPS) as i:
                step(i, False)
            output(2 * PAIRS - 1, 1, False)

            def turn(i, s, first):
                h = i * NX + s
                pe.wait_ge(c_loaded[s], 16 * (i + 1))
                for q in range(2):
                    if not (first and s == 0):
                        pe.wait_ge(u_split, 2 * (h - 1) + q + 1)
                    for b in range(NB // 2):
                        k = q * (NB // 2) + b
                        ins = nc.tensor.transpose(turn_bank(q)[:, b * P:(b + 1) * P], xt[:, s, k * P:(k + 1) * P], ident[:])
                    ins.then_inc(turned, 1)

            def conv(i, s, first):
                h = i * NX + s
                pe.wait_ge(t_loaded[s % NT], 16 * (i + 1))
                pe.wait_ge(u_split, 2 * h + 2)
                if not (first and s < 2):
                    pe.wait_ge(y_scaled, h - 1)
                y = y_banks(s)
                for k in range(NB):
                    for u, half in ((u_hi, 0), (u_hi, 1), (u_lo, 0)):
                        for bank in range(2):
                            begin, end = bank * HALF, min(T - k * P, (bank + 1) * HALF)
                            if begin >= end:
                                continue
                            ins = M(y[:, begin:end], u[:, s % 2, k, :], toep[:, s % NT, half, k * P + begin:k * P + end],
                                    start=(k == 0 and u is u_hi and half == 0),
                                    stop=(k == NB - 1 - bank * NB // 2 and u is u_lo))
                ins.then_inc(conv_done, 1)

            def step2(i, first, last):
                for s in range(NX):
                    if s < NX - 1:
                        turn(i, s + 1, first)
                    elif not last:
                        turn(i + 1, 0, False)
                    conv(i, s, first)

            pe.wait_ge(x1_ready, 2 * PAIRS)
            pe.wait_ge(mask_ready, 1)
            turn(0, 0, True)
            step2(0, True, False)
            with pe.Fori(1, CSTEPS - 1) as i:
                step2(i, False, False)
            step2(CSTEPS - 1, False, True)


_INS = ['x', 'itok_B_0_7', 'itok_B_2182_4065', 'itok_B_78_3631', '_lenS', 'L0_cond_W_sess', 'L0_cond_b_sess',
        'L0_cond_W2', 'L0_cond_b2', 'L1_cond_log_dt', 'L1_cond_C', 'L1_cond_log_A_real', 'L1_cond_A_imag', 'L1_cond_D']
_OUTS = [((128, 64, 1024), 'float32')]


def kernel(**inputs):
    import numpy as _np
    import concourse.bacc as _bacc
    from concourse import mybir as _mybir
    from concourse.bass_utils import run_bass_kernel_spmd as _run

    nc = _bacc.Bacc("TRN2", target_bir_lowering=False, num_devices=1)
    arrays, args = {}, []
    for name in _INS:
        a = _np.ascontiguousarray(inputs[name])
        arrays[f"in_{name}_dram"] = a
        args.append(nc.dram_tensor(f"in_{name}_dram", a.shape, _mybir.dt.from_np(a.dtype), kind="ExternalInput").ap())
    for i, (shape, dtype) in enumerate(_OUTS):
        dt = _mybir.dt.from_np(_np.dtype(dtype))
        args.append(nc.dram_tensor(f"out_{i}_dram", shape, dt, kind="ExternalOutput").ap())
    build_cond_residual(nc, *args)
    r = _run(nc, [arrays], core_ids=[0])
    got = tuple(r.results[0][f"out_{i}_dram"] for i in range(len(_OUTS)))
    return got[0]
```

```python
import math
from contextlib import ExitStack

import concourse.bass as bass
from concourse import mybir

ALU = mybir.AluOpType
ACT = mybir.ActivationFunctionType
AX_X = mybir.AxisListType.X
F32 = mybir.dt.float32
F16 = mybir.dt.float16
I32 = mybir.dt.int32

P = 128
SCALE = 256.0
UNSCALE = 1.0 / (SCALE * SCALE)
MAGIC = 12582912.0
TWO_PI_PARTS = (6.28125, 0.0019353071795864769)
LN2_PARTS = (0.693359375, -2.12194440054691e-04)
HALF_PI = math.pi / 2
PI_BELOW = 3.1415925


def build_cond_residual(
    nc: bass.Bass,
    x: bass.AP,
    session_ids: bass.AP,
    seq_lens: bass.AP,
    conv_lens: bass.AP,
    channel_counts: bass.AP,
    W_sess: bass.AP,
    b_sess: bass.AP,
    W2: bass.AP,
    b2: bass.AP,
    log_dt: bass.AP,
    C: bass.AP,
    log_A_real: bass.AP,
    A_imag: bass.AP,
    D: bass.AP,
    out: bass.AP,
):
    B, H, T = x.shape
    S, _, HID = W_sess.shape
    N = A_imag.shape[1]
    assert B == P and HID == P and 2 * H == P and 2 * N == P
    HALF = T // 2
    PAIRS = B // 2
    NB = T // P
    TA = TB = 32
    LOW, HIGH = 4, 8
    TIMES = 2 * (LOW + HIGH)
    assert TA * TB == T and HALF == 512 and LOW * HIGH == TA == TB
    KROW = T + P

    x1_dram = nc.dram_tensor("x1_scratch", (H, B, T), F32).ap()
    k_scratch = nc.dram_tensor("k_halves", (2, H, KROW), F16)
    k_dram = k_scratch.ap()

    NX = 8
    NS = 4
    NT = 4
    AHEAD = 2

    with ExitStack() as ctx:
        def sb(name, shape, dt):
            return ctx.enter_context(nc.sbuf_tensor(name, shape, dt))

        def sem(name):
            return ctx.enter_context(nc.semaphore(name))

        psum = ctx.enter_context(nc.psum_tensor("psum", [P, 8, HALF], F32))

        ident = sb("ident", [P, P], F32)
        iota_t = sb("iota_t", [P, T], F32)
        chan_of_part = sb("chan_of_part", [P, 1], F32)
        part_index = sb("part_index", [P, 1], F32)
        sid_i = sb("sid_i", [P, B], I32)
        cnt_i = sb("cnt_i", [P, B], I32)
        seq_i = sb("seq_i", [P, B], I32)
        len_i = sb("len_i", [P, 1], I32)
        sid_f = sb("sid_f", [P, B], F32)
        cnt_f = sb("cnt_f", [P, B], F32)
        seq_f = sb("seq_f", [P, B], F32)
        seq_pair = sb("seq_pair", [P, PAIRS], F32)
        len_f = sb("len_f", [P, 1], F32)
        live = sb("live", [P, B], F32)
        w_offset_f = sb("w_offset_f", [1, B], F32)
        w_offset = sb("w_offset", [1, B], I32)
        channel_scale = sb("channel_scale", [P, PAIRS], F32)
        scale_now = sb("scale_now", [P, NX], F32)
        onehot = sb("onehot", [S, B], F32)
        bs_sb = sb("bs_sb", [S, HID], F32)
        bias_all = sb("bias_all", [P, B], F32)
        w2_sb = sb("w2_sb", [P, H], F32)
        b2_col = sb("b2_col", [P, 1], F32)
        seq_min = sb("seq_min", [1, 2], F32)
        seq_min_i = sb("seq_min_i", [1, 1], I32)
        ws_raw = sb("ws_raw", [P, S, HID], F32)
        w_tab = sb("w_tab", [P, S, 2, HID], F16)
        zeros16 = sb("zeros16", [H, P], F16)

        par = sb("par", [H, 4 * N], F32)
        par2 = sb("par2", [H, 4, 2, N], F32)
        parT = sb("parT", [P, 4, H], F32)
        ex = sb("ex", [P, 2, H], F32)
        small = sb("small", [P, 28, H], F32)
        expo = sb("expo", [P, 4, H], F32)
        times = sb("times", [P, TIMES], F32)
        tab_im = sb("tab_im", [P, H, TIMES], F32)
        tab_re = sb("tab_re", [P, H, TIMES], F32)
        tab_c = sb("tab_c", [P, H, TIMES], F32)
        tab_k = sb("tab_k", [P, H, TIMES], F32)
        low = sb("low", [P, 4, H, LOW], F32)
        gmat = sb("gmat", [P, H, TA], F32)
        emat = sb("emat", [P, H, TB], F32)
        outer = sb("outer", [P, H, TA], F32)
        is_top = sb("is_top", [P, 1], F32)
        is_bottom = sb("is_bottom", [P, 1], F32)
        k_hi = sb("k_hi", [TA, H, TB], F16)
        k_lo = sb("k_lo", [TA, H, TB], F16)
        d_all = sb("d_all", [TA, H], F32)
        is_last = sb("is_last", [TA, 1], F32)
        d_last = sb("d_last", [TA, H], F32)

        xt = sb("xt", [P, NX, T], F32)
        xs = sb("xs", [P, NS, 2, T], F16)
        hid = sb("hid", [P, 2, 2, T], F32)
        tmp = sb("tmp", [P, T], F32)

        toep = sb("toep", [P, NT, 2, T], F16)
        u_hi = sb("u_hi", [P, 2, NB, P], F16)
        u_lo = sb("u_lo", [P, 2, NB, P], F16)
        ys = sb("ys", [P, 2, T], F32)

        s_ids = sem("s_ids")
        s_par = sem("s_par")
        s_wraw = sem("s_wraw")
        s_small = sem("s_small")
        s_iota = sem("s_iota")
        s_ident0 = sem("s_ident0")
        s_ident = sem("s_ident")
        s_chain = sem("s_chain")
        s_onehot = sem("s_onehot")
        s_biasmm = sem("s_biasmm")
        s_bias = sem("s_bias")
        s_zeros = sem("s_zeros")
        s_offset = sem("s_offset")
        s_scale = sem("s_scale")
        s_wsplit = sem("s_wsplit")
        s_par2 = sem("s_par2")
        s_parT = sem("s_parT")
        s_tables = sem("s_tables")
        s_coef = sem("s_coef")
        s_pool = sem("s_pool")
        s_parC = sem("s_parC")
        s_ang = sem("s_ang")
        s_trig = sem("s_trig")
        s_gmat = sem("s_gmat")
        s_kmm = sem("s_kmm")
        s_ksplit = sem("s_ksplit")
        s_kstored = sem("s_kstored")

        x_loaded = [sem(f"x_loaded{n}") for n in range(NX)]
        x1_stored = [sem(f"x1_stored{n}") for n in range(NX)]
        scale_copied = sem("scale_copied")
        hi_by_act = [sem(f"hi_by_act{j}") for j in range(2)]
        hi_by_pool = sem("hi_by_pool")
        x_split = sem("x_split")
        h_ready = sem("h_ready")
        gelu_done = sem("gelu_done")
        o_ready = sem("o_ready")
        x1_ready = sem("x1_ready")
        t_loaded = [sem(f"t_loaded{n}") for n in range(NT)]
        c_loaded = [sem(f"c_loaded{n}") for n in range(NX)]
        out_stored = [sem(f"out_stored{n}") for n in range(NX)]
        turned = sem("turned")
        u_hi_done = sem("u_hi_done")
        u_split = sem("u_split")
        conv_done = sem("conv_done")
        y_scaled = sem("y_scaled")
        out_ready = sem("out_ready")
        mask_ready = sem("mask_ready")
        act_passed = sem("act_passed")
        pool_passed = sem("pool_passed")
        dve_passed = sem("dve_passed")
        tmp_done = sem("tmp_done")

        def hid_banks(j):
            return psum[:, 2 * j:2 * j + 2, :]

        def mlp_banks(s):
            return psum[:, 4 + 2 * (s % 2):6 + 2 * (s % 2), :]

        def flat(banks):
            return banks.rearrange("p a n -> p (a n)")

        def turn_bank(q):
            return psum[:, q, :]

        def y_banks(h):
            return psum[:, 2 + 2 * (h % 2):4 + 2 * (h % 2), :].rearrange("p a n -> p (a n)")

        mask = psum[:, 6:8, :].rearrange("p a n -> p (a n)")

        small_col = {}

        def sm(name):
            if name not in small_col:
                small_col[name] = len(small_col)
            return small[:, small_col[name], :]

        kpsum = psum[0:TA, 4:8, :].rearrange("p a n -> p (a n)").rearrange("p (h b) -> p h b", b=TB)


        STEPS = PAIRS // NX
        K_STEP = 5
        POOL_TURN = 4
        POOL_PAIR = POOL_TURN * NX
        CSTEPS = H // NX

        block = ctx.enter_context(nc.Block())

        @block.sync
        def _(sp):
            for j in range(2):
                sp.dma_start(ws_raw[j * H:(j + 1) * H, :, :], W_sess.rearrange("s c d -> c s d")).then_inc(s_wraw, 16)
            def load_x(p, slot):
                sp.dma_start(xt[:, slot, :], x[bass.ds(2 * p, 2)].rearrange("b c t -> (b c) t")).then_inc(x_loaded[slot], 16)

            def store_x1(p, slot):
                for j in range(2):
                    sp.dma_start(x1_dram[:, bass.ds(2 * p + j, 1), :].rearrange("c b t -> (c b) t"),
                                 xt[j * H:(j + 1) * H, slot, :]).then_inc(x1_stored[slot], 16)

            def stage1_step(i, first, last):
                for s in range(NX):
                    p = i * NX + s
                    sp.wait_ge(x1_ready, p + 1)
                    store_x1(p, s)
                    if not (last and s > 0):
                        nxt = (s + NX - 1) % NX
                        if not (first and s == 0):
                            sp.wait_ge(x1_stored[nxt], 32 * (i + (1 if s > 0 else 0)))
                            load_x(p + NX - 1, nxt)

            def store_kernel():
                sp.wait_ge(s_zeros, 1)
                sp.wait_ge(s_ksplit, 2)
                for half, src in enumerate((k_hi, k_lo)):
                    sp.dma_start(k_dram[half, :, 0:T].rearrange("h (a b) -> a h b", b=TB), src[:]).then_inc(s_kstored, 16)
                    sp.dma_start(k_dram[half, :, T:KROW], zeros16[:]).then_inc(s_kstored, 16)

            for s in range(NX):
                load_x(s, s)
            stage1_step(0, True, False)
            with sp.Fori(1, K_STEP + 1) as i:
                stage1_step(i, False, False)
            store_kernel()
            with sp.Fori(K_STEP + 1, STEPS - 1) as i:
                stage1_step(i, False, False)
            stage1_step(STEPS - 1, False, True)

            def load_toeplitz(h, slot):
                row = k_dram[:, bass.ds(h, 1), :]
                sp.dma_start(toep[:, slot % NT, :, :], bass.AP(k_scratch, row.offset, [[1, P], [H * KROW, 2], [1, T]])
                             ).then_inc(t_loaded[slot % NT], 16)

            def load_channel(h, slot):
                sp.dma_start(xt[:, slot, :], x1_dram[bass.ds(h, 1)].rearrange("a b t -> (a b) t")).then_inc(c_loaded[slot], 16)

            def store_out(h, slot):
                sp.dma_start(out[:, bass.ds(h, 1), :].rearrange("b a t -> (b a) t"), xt[:, slot, :]).then_inc(out_stored[slot], 16)

            def stage2_step(i, first, last):
                for s in range(NX):
                    h = i * NX + s
                    sp.wait_ge(out_ready, h + 1)
                    store_out(h, s)
                    if not (last and s > 0) and not (first and s == 0):
                        nxt = (s + NX - 1) % NX
                        sp.wait_ge(out_stored[nxt], 16 * (i + (1 if s > 0 else 0)))
                        load_channel(h + NX - 1, nxt)
                    if not (last and s + NT >= NX):
                        load_toeplitz(h + NT, s)

            sp.wait_ge(s_kstored, 64)
            for s in range(NT):
                load_toeplitz(s, s)
            for s in range(NX):
                sp.wait_ge(x1_stored[s], 32 * STEPS)
            for s in range(NX):
                load_channel(s, s)
            stage2_step(0, True, False)
            with sp.Fori(1, CSTEPS - 1) as i:
                stage2_step(i, False, False)
            stage2_step(CSTEPS - 1, False, True)
            for s in range(NX):
                sp.wait_ge(out_stored[s], 16 * CSTEPS)

        @block.gpsimd
        def _(pool):
            nc.gpsimd.iota(iota_t[:], pattern=[[1, T]], base=0, channel_multiplier=0,
                           allow_small_or_imprecise_dtypes=True).then_inc(s_iota, 1)
            at = 0
            for unit in (1, TB):
                for step_, n in ((unit, LOW), (unit * LOW, HIGH)):
                    nc.gpsimd.iota(times[:, at:at + n], pattern=[[-step_, n]], base=step_ * (n - 1), channel_multiplier=0,
                                   allow_small_or_imprecise_dtypes=True).then_inc(s_iota, 1)
                    at += n
            nc.gpsimd.iota(part_index[:], pattern=[[0, 1]], base=0, channel_multiplier=1,
                           allow_small_or_imprecise_dtypes=True).then_inc(s_iota, 1)
            nc.gpsimd.memset(ident[:], 0.0).then_inc(s_ident0, 1)
            pool.wait_ge(s_ident0, 1)
            nc.gpsimd.affine_select(out=ident[:], in_=ident[:], compare_op=ALU.not_equal, fill=1.0, base=0,
                                    pattern=[[-1, P]], channel_multiplier=1).then_inc(s_ident, 1)

            done = [0]

            def link(ins):
                done[0] += 1
                ins.then_inc(s_pool, 1)
                pool.wait_ge(s_pool, done[0])

            mul = lambda o, a, b: nc.gpsimd.tensor_tensor(o, a, b, ALU.mult)
            add = lambda o, a, b: nc.gpsimd.tensor_tensor(o, a, b, ALU.add)
            line = lambda o, a, m, c: nc.gpsimd.tensor_scalar(o, a, m, c, ALU.mult, ALU.add)

            def over_times(v):
                return (v.unsqueeze(2).to_broadcast([P, H, TIMES]), times[:].unsqueeze(1).to_broadcast([P, H, TIMES]))

            pool.wait_ge(s_ang, 1)
            mul(tab_re[:], *over_times(sm("re")))
            link(mul(tab_im[:], *over_times(sm("im"))))
            link(line(tab_k[:], tab_im[:], 1.0 / (2.0 * math.pi), MAGIC))
            link(nc.gpsimd.tensor_scalar(tab_k[:], tab_k[:], -MAGIC, -TWO_PI_PARTS[0], ALU.add, ALU.mult))
            link(add(tab_im[:], tab_im[:], tab_k[:]))
            link(nc.gpsimd.tensor_scalar(tab_k[:], tab_k[:], TWO_PI_PARTS[1] / TWO_PI_PARTS[0], 1.0, ALU.mult, ALU.mult))
            link(add(tab_im[:], tab_im[:], tab_k[:]))
            nc.gpsimd.tensor_scalar(tab_im[:], tab_im[:], PI_BELOW, -PI_BELOW, ALU.min, ALU.max).then_inc(s_tables, 1)

            pool.wait_ge(s_trig, 6)
            link(mul(tab_c[:], tab_c[:], tab_c[:]))
            mul(tab_im[:], tab_im[:], tab_re[:])
            link(line(tab_c[:], tab_c[:], -2.0, 1.0))
            link(mul(tab_c[:], tab_c[:], tab_re[:]))
            b_low, b_high, a_low, a_high = (slice(0, LOW), slice(LOW, LOW + HIGH), slice(LOW + HIGH, 2 * LOW + HIGH),
                                            slice(2 * LOW + HIGH, TIMES))
            scaled = lambda o, a, m: nc.gpsimd.tensor_scalar(o, a, m, 1.0, ALU.mult, ALU.mult)
            u, v, w, z = (low[:, k] for k in range(4))

            def over_high(dst, high):
                shape = [P, H, HIGH, LOW]
                spread_low = lambda t: t.unsqueeze(2).to_broadcast(shape)
                spread_high = lambda t: t[:, :, high].unsqueeze(3).to_broadcast(shape)
                split = lambda t: t.rearrange("p h (x y) -> p h x y", y=LOW)
                mul(split(dst), spread_low(u), spread_high(tab_c))
                link(mul(split(outer[:]), spread_low(v), spread_high(tab_im)))
                return add(dst, dst, outer[:])

            scaled(u, tab_c[:, :, b_low], is_top[:, 0:1])
            scaled(w, tab_im[:, :, b_low], is_bottom[:, 0:1])
            scaled(v, tab_c[:, :, b_low], is_bottom[:, 0:1])
            link(scaled(z, tab_im[:, :, b_low], is_top[:, 0:1]))
            add(u, u, w)
            link(nc.gpsimd.tensor_tensor(v, v, z, ALU.subtract))
            link(over_high(emat[:], b_high))
            pool.wait_ge(s_coef, 1)
            per_mode = lambda t: sm(t).unsqueeze(2).to_broadcast([P, H, LOW])
            mul(u, tab_c[:, :, a_low], per_mode("gp"))
            mul(w, tab_im[:, :, a_low], per_mode("gq"))
            mul(v, tab_c[:, :, a_low], per_mode("gq"))
            link(mul(z, tab_im[:, :, a_low], per_mode("gp")))
            add(u, u, w)
            link(nc.gpsimd.tensor_tensor(v, v, z, ALU.subtract))
            over_high(gmat[:], a_high).then_inc(s_gmat, 1)
            pool.wait_ge(s_gmat, 1)

            def copy_scales(i):
                nc.gpsimd.tensor_copy(scale_now[:], channel_scale[:, bass.ds(i * NX, NX)]).then_inc(scale_copied, 1)

            def split_hi(i, s):
                p = i * NX + s
                pool.wait_ge(x_loaded[s], 16 * (i + 1))
                pool.wait_ge(h_ready, 2 * (p - NS) + 2)
                if s == 0:
                    pool.wait_ge(scale_copied, i - POOL_TURN + 1)
                pool.sem_inc(pool_passed, 1)
                nc.gpsimd.tensor_scalar(xs[H:P, s % NS, 1, :], xt[H:P, s, :], scale_now[H:P, s:s + 1], 1.0,
                                        ALU.mult, ALU.mult).then_inc(hi_by_pool, 1)

            def step(i, first):
                if not first:
                    pool.wait_ge(hi_by_pool, NX * i - POOL_PAIR)
                copy_scales(i)
                for s in range(NX):
                    split_hi(i, s)

            step(POOL_TURN, True)
            with pool.Fori(POOL_TURN + 1, STEPS) as i:
                step(i, False)

        @block.scalar
        def _(act):
            for ap, src in ((par[:, 0:N], log_A_real), (par[:, N:2 * N], A_imag),
                            (par[:, 2 * N:4 * N], C.rearrange("h n z -> h (n z)")), (ex[:, 0, :], log_dt.partition_broadcast(P))):
                act.dma_start(ap, src).then_inc(s_par, 16)
            for ap, src in ((sid_i, session_ids), (cnt_i, channel_counts), (seq_i, seq_lens)):
                act.dma_start(ap[:], src.partition_broadcast(P)).then_inc(s_ids, 16)
            act.dma_start(len_i[:], conv_lens.rearrange("(b a) -> b a", a=1)).then_inc(s_ids, 16)
            act.dma_start(bs_sb[:], b_sess).then_inc(s_small, 16)
            act.dma_start(w2_sb[:], W2).then_inc(s_small, 16)
            for j in range(2):
                act.dma_start(b2_col[j * H:(j + 1) * H, :], b2.rearrange("(s a) -> s a", a=1)).then_inc(s_small, 16)
            act.dma_start(d_all[:], D.partition_broadcast(TA)).then_inc(s_small, 16)

            def split_hi(i, s, j, first):
                p = i * NX + s
                q = slice(j * H, (j + 1) * H)
                act.wait_ge(x_loaded[s], 16 * (i + 1))
                if not (first and s < NS):
                    act.wait_ge(h_ready, 2 * (p - NS) + 2)
                act.sem_inc(act_passed, 1)
                nc.scalar.activation(xs[q, s % NS, j, :], xt[q, s, :], ACT.Copy,
                                     scale=channel_scale[q, bass.ds(p, 1)]).then_inc(hi_by_act[j], 1)

            def step(i, first, last):
                for s in range(NX):
                    p = i * NX + s
                    for j in range(2):
                        act.wait_ge(h_ready, 2 * p + j + 1)
                        if j == 0 and not (first and s < 2):
                            act.wait_ge(o_ready, p - 1)
                        act.sem_inc(act_passed, 1)
                        nc.scalar.activation(hid[:, s % 2, j, :], flat(hid_banks(j)), ACT.Gelu,
                                             bias=bias_all[:, bass.ds(2 * p + j, 1)],
                                             scale=UNSCALE).then_inc(gelu_done, 1)
                        over, slot = divmod(s + AHEAD + 1, NX)
                        static = isinstance(i, int)
                        if not (last and over) and (j == 0 or static and p + AHEAD + 1 < POOL_PAIR):
                            split_hi(i + over, slot, j, first and not over)

            act.wait_ge(s_scale, 1)
            for s in range(AHEAD + 1):
                for j in range(2):
                    split_hi(0, s, j, True)
            act.wait_ge(s_bias, 1)
            step(0, True, False)
            step(1, False, False)
            act.wait_ge(s_ang, 1)
            nc.scalar.activation(sm("t_step"), sm("t_step_arg"), ACT.Tanh).then_inc(s_trig, 1)
            act.wait_ge(s_tables, 1)
            nc.scalar.activation(tab_re[:], tab_re[:], ACT.Exp).then_inc(s_trig, 1)
            nc.scalar.activation(sm("sin_half"), sm("half_arg"), ACT.Sin).then_inc(s_trig, 1)
            nc.scalar.activation(sm("cos_half"), sm("half_arg_c"), ACT.Sin).then_inc(s_trig, 1)
            nc.scalar.activation(tab_c[:], tab_im[:], ACT.Sin, scale=0.5).then_inc(s_trig, 1)
            nc.scalar.activation(tab_im[:], tab_im[:], ACT.Sin).then_inc(s_trig, 1)
            for i in range(2, POOL_TURN):
                step(i, False, False)
            with act.Fori(POOL_TURN, STEPS - 1) as i:
                step(i, False, False)
            step(STEPS - 1, False, True)

            def split_hi(i, s, first):
                h = i * NX + s
                for q in range(2):
                    act.wait_ge(turned, 2 * h + q + 1)
                    if q == 0 and not (first and s < 2):
                        act.wait_ge(conv_done, h - 1)
                    nc.scalar.activation(u_hi[:, s % 2, q * (NB // 2):(q + 1) * (NB // 2), :].rearrange("p k b -> p (k b)"),
                                         turn_bank(q), ACT.Copy, scale=SCALE).then_inc(u_hi_done, 1)

            def unscale(h, s, first):
                act.wait_ge(conv_done, h + 1)
                if not (first and s < 2):
                    act.wait_ge(out_ready, h - 1)
                y = y_banks(s)
                nc.scalar.activation(ys[:, s % 2, :], bass.AP(y.tensor, y.offset + T - 1, [y.ap[0], [-1, T]]), ACT.Copy, scale=UNSCALE).then_inc(y_scaled, 1)

            def step2(i, first, last):
                for s in range(NX):
                    if s < NX - 1:
                        split_hi(i, s + 1, first)
                    elif not last:
                        split_hi(i + 1, 0, False)
                    unscale(i * NX + s, s, first)

            split_hi(0, 0, True)
            step2(0, True, False)
            with act.Fori(1, CSTEPS - 1) as i:
                step2(i, False, False)
            step2(CSTEPS - 1, False, True)

        @block.vector
        def _(dve):
            chain = [0]

            def link(ins):
                chain[0] += 1
                ins.then_inc(s_chain, 1)
                dve.wait_ge(s_chain, chain[0])

            V = nc.vector
            V.memset(zeros16[:], 0.0).then_inc(s_zeros, 1)

            dve.wait_ge(s_par, 64)
            c_parts = par[:, 2 * N:4 * N].rearrange("h (n z) -> h n z", z=2)
            for k, v in enumerate((par[:, 0:N], par[:, N:2 * N], c_parts[:, :, 0], c_parts[:, :, 1])):
                ins = V.tensor_copy(par2[:, k], v.unsqueeze(1).to_broadcast([H, 2, N]))
            ins.then_inc(s_par2, 1)

            dve.wait_ge(s_ids, 64)
            dve.wait_ge(s_iota, 6)
            V.tensor_copy(chan_of_part[0:H, :], part_index[0:H, :])
            V.tensor_scalar(chan_of_part[H:P, :], part_index[H:P, :], float(-H), None, ALU.add)
            V.tensor_copy(sid_f[:], sid_i[:])
            V.tensor_copy(cnt_f[:], cnt_i[:])
            V.tensor_copy(len_f[:], len_i[:])
            link(V.tensor_copy(seq_f[:], seq_i[:]))
            for j in range(2):
                q = slice(j * H, (j + 1) * H)
                V.tensor_copy(seq_pair[q, :], seq_f[q, :].rearrange("p (n j) -> p n j", j=2)[:, :, j])
            link(V.tensor_reduce(seq_min[:, 0:1], seq_f[0:1, :], AX_X, ALU.min))
            link(V.tensor_copy(seq_min_i[:], seq_min[:, 0:1]))
            V.tensor_scalar(onehot[:], sid_f[0:S, :], part_index[0:S, 0:1], None, ALU.is_equal).then_inc(s_onehot, 1)
            V.tensor_scalar(w_offset_f[:], sid_f[0:1, :], float(S - 1), 0.0, ALU.min, ALU.max)
            link(V.tensor_scalar(live[:], cnt_f[:], chan_of_part[:, 0:1], SCALE, ALU.is_gt, ALU.mult))
            V.tensor_scalar(w_offset[:], w_offset_f[:], 2.0 * HID, None, ALU.mult).then_inc(s_offset, 1)
            for j in range(2):
                q = slice(j * H, (j + 1) * H)
                ins = V.tensor_copy(channel_scale[q, :], live[q, :].rearrange("p (n j) -> p n j", j=2)[:, :, j])
            ins.then_inc(s_scale, 1)
            dve.wait_ge(s_wraw, 32)
            link(V.tensor_scalar(w_tab[:, :, 0, :], ws_raw[:], SCALE, None, ALU.mult))
            V.scalar_tensor_tensor(out=w_tab[:, :, 1, :], in0=ws_raw[:], scalar=SCALE, in1=w_tab[:, :, 0, :],
                                   op0=ALU.mult, op1=ALU.subtract).then_inc(s_wsplit, 1)
            dve.wait_ge(s_biasmm, 1)
            V.tensor_copy(bias_all[:], psum[:, 7, 0:B]).then_inc(s_bias, 1)

            V.tensor_scalar(is_bottom[:], part_index[:], float(N), None, ALU.is_ge)
            V.tensor_scalar(is_top[:], part_index[:], float(N), None, ALU.is_lt)
            V.tensor_scalar(is_last[:], part_index[0:TA, :], float(TA - 1), None, ALU.is_equal)

            dve.wait_ge(s_parT, 1)
            V.tensor_copy(parT[:], psum[:, 6, 0:4 * H].rearrange("p (k h) -> p k h", k=4)).then_inc(s_parC, 1)
            dve.wait_ge(s_parC, 1)
            dve.wait_ge(s_par, 64)
            link(V.tensor_copy(ex[:, 1, :], parT[:, 0, :]))
            v = ex[:]
            k = expo[:, 0:2, :]
            acc = expo[:, 2:4, :]
            link(V.tensor_scalar(k, v, 1.0 / math.log(2.0), MAGIC, ALU.mult, ALU.add))
            link(V.tensor_scalar(k, k, -MAGIC, None, ALU.add))
            for part in LN2_PARTS:
                link(V.scalar_tensor_tensor(out=v, in0=k, scalar=-part, in1=v, op0=ALU.mult, op1=ALU.add))
            link(V.tensor_scalar(acc, v, 1.0 / math.factorial(7), 1.0 / math.factorial(6), ALU.mult, ALU.add))
            for n in range(5, -1, -1):
                link(V.tensor_tensor(acc, acc, v, ALU.mult))
                link(V.tensor_scalar(acc, acc, 1.0 / math.factorial(n), None, ALU.add))
            link(V.tensor_scalar(v.bitcast(I32), k, 127.0, float(1 << 23), ALU.add, ALU.mult))
            link(V.tensor_tensor(ex[:], acc, v, ALU.mult))
            dt, rate = ex[:, 0, :], ex[:, 1, :]
            a_im, c_re, c_im = parT[:, 1, :], parT[:, 2, :], parT[:, 3, :]
            V.tensor_tensor(sm("im"), a_im, dt, ALU.mult)
            V.tensor_scalar(sm("a_re"), rate, -1.0, None, ALU.mult)
            link(V.tensor_tensor(sm("re0"), rate, dt, ALU.mult))
            link(V.tensor_scalar(sm("re"), sm("re0"), -1.0, None, ALU.mult))

            def reduce_angle(ang, k):
                link(V.tensor_scalar(k, ang, 1.0 / (2.0 * math.pi), MAGIC, ALU.mult, ALU.add))
                link(V.tensor_scalar(k, k, -MAGIC, None, ALU.add))
                for part in TWO_PI_PARTS:
                    link(V.scalar_tensor_tensor(out=ang, in0=k, scalar=-part, in1=ang, op0=ALU.mult, op1=ALU.add))
                link(V.tensor_scalar(ang, ang, PI_BELOW, -PI_BELOW, ALU.min, ALU.max))

            def cosine_argument(dst, ang):
                link(V.scalar_tensor_tensor(out=dst, in0=ang, scalar=-1.0, in1=ang, op0=ALU.mult, op1=ALU.min))
                return V.tensor_scalar(dst, dst, HALF_PI, None, ALU.add)

            link(V.tensor_copy(sm("step"), sm("im")))
            reduce_angle(sm("step"), sm("k1"))
            link(V.tensor_scalar(sm("half_arg"), sm("step"), 0.5, None, ALU.mult))
            link(cosine_argument(sm("half_arg_c"), sm("half_arg")))
            V.tensor_scalar(sm("t_step_arg"), sm("re"), 0.5, None, ALU.mult).then_inc(s_ang, 1)

            def coefficients():
                dve.wait_ge(s_trig, 4)
                V.tensor_scalar(sm("one_minus_t"), sm("t_step"), -1.0, 1.0, ALU.mult, ALU.add)
                V.tensor_tensor(sm("sin2"), sm("sin_half"), sm("sin_half"), ALU.mult)
                V.tensor_tensor(sm("sincos"), sm("sin_half"), sm("cos_half"), ALU.mult)
                V.tensor_tensor(sm("abs2"), sm("a_re"), sm("a_re"), ALU.mult)
                link(V.tensor_tensor(sm("aim2"), a_im, a_im, ALU.mult))
                V.reciprocal(sm("k1"), sm("one_minus_t"))
                link(V.tensor_tensor(sm("abs2"), sm("abs2"), sm("aim2"), ALU.add))
                V.tensor_tensor(sm("em1"), sm("k1"), sm("t_step"), ALU.mult)
                V.tensor_scalar(sm("aim2"), sm("sin2"), -2.0, 1.0, ALU.mult, ALU.add)
                link(V.reciprocal(sm("inv"), sm("abs2")))
                V.tensor_scalar(sm("k1"), sm("em1"), 2.0, 1.0, ALU.mult, ALU.add)
                link(V.tensor_tensor(sm("er"), sm("em1"), sm("aim2"), ALU.mult))
                V.tensor_tensor(sm("er"), sm("er"), sm("sin2"), ALU.subtract)
                link(V.tensor_tensor(sm("ei"), sm("k1"), sm("sincos"), ALU.mult))
                V.tensor_tensor(sm("zr"), sm("er"), sm("a_re"), ALU.mult)
                V.tensor_tensor(sm("k1"), sm("ei"), a_im, ALU.mult)
                V.tensor_tensor(sm("zi"), sm("ei"), sm("a_re"), ALU.mult)
                link(V.tensor_tensor(sm("sin2"), sm("er"), a_im, ALU.mult))
                V.tensor_tensor(sm("zr"), sm("zr"), sm("k1"), ALU.add)
                V.tensor_tensor(sm("zi"), sm("zi"), sm("sin2"), ALU.subtract)
                link(V.tensor_scalar(sm("inv"), sm("inv"), 4.0, None, ALU.mult))
                V.tensor_tensor(sm("zr"), sm("zr"), sm("inv"), ALU.mult)
                link(V.tensor_tensor(sm("zi"), sm("zi"), sm("inv"), ALU.mult))
                V.tensor_tensor(sm("k1"), c_re, sm("zr"), ALU.mult)
                V.tensor_tensor(sm("er"), c_im, sm("zi"), ALU.mult)
                V.tensor_tensor(sm("ei"), c_re, sm("zi"), ALU.mult)
                link(V.tensor_tensor(sm("sin2"), c_im, sm("zr"), ALU.mult))
                V.tensor_tensor(sm("er"), sm("k1"), sm("er"), ALU.subtract)
                link(V.tensor_tensor(sm("ei"), sm("ei"), sm("sin2"), ALU.add))
                V.tensor_scalar(sm("k1"), sm("er"), is_top[:, 0:1], None, ALU.mult)
                V.tensor_scalar(sm("aim2"), sm("ei"), is_top[:, 0:1], -1.0, ALU.mult, ALU.mult)
                V.tensor_scalar(sm("gp"), sm("ei"), is_bottom[:, 0:1], -1.0, ALU.mult, ALU.mult)
                link(V.tensor_scalar(sm("gq"), sm("er"), is_bottom[:, 0:1], -1.0, ALU.mult, ALU.mult))
                V.tensor_tensor(sm("gp"), sm("gp"), sm("k1"), ALU.add)
                V.tensor_tensor(sm("gq"), sm("gq"), sm("aim2"), ALU.add).then_inc(s_coef, 1)

            def split_kernel():
                dve.wait_ge(s_small, 80)
                link(V.tensor_scalar(d_last[:], d_all[:], 1.0, is_last[:, 0:1], ALU.add, ALU.mult))
                dve.wait_ge(s_kmm, 1)
                link(V.tensor_tensor(kpsum[:, :, TB - 1], kpsum[:, :, TB - 1], d_last[:], ALU.add))
                V.tensor_scalar(k_hi[:], kpsum, SCALE, None, ALU.mult).then_inc(s_ksplit, 1)
                dve.wait_ge(s_ksplit, 1)
                V.scalar_tensor_tensor(out=k_lo[:].rearrange("p h b -> p (h b)"), in0=kpsum.rearrange("p h b -> p (h b)"),
                                       scalar=SCALE, in1=k_hi[:].rearrange("p h b -> p (h b)"),
                                       op0=ALU.mult, op1=ALU.subtract).then_inc(s_ksplit, 1)

            def split_lo(i, s, by_pool):
                p = i * NX + s
                for j in range(2):
                    q = slice(j * H, (j + 1) * H)
                    other = slice((1 - j) * H, (2 - j) * H)
                    if j == 1 and by_pool:
                        dve.wait_ge(hi_by_pool, p - POOL_PAIR + 1)
                    else:
                        dve.wait_ge(hi_by_act[j], p + 1)
                    V.scalar_tensor_tensor(out=xs[other, s % NS, j, :], in0=xt[q, s, :],
                                           scalar=channel_scale[q, bass.ds(p, 1)],
                                           in1=xs[q, s % NS, j, :], op0=ALU.mult, op1=ALU.subtract).then_inc(x_split, 1)

            def add_mlp(i, s, masked):
                p = i * NX + s
                dve.wait_ge(o_ready, p + 1)
                if not masked:
                    V.scalar_tensor_tensor(out=xt[:, s, :], in0=flat(mlp_banks(s)), scalar=b2_col[:, 0:1],
                                           in1=xt[:, s, :], op0=ALU.add, op1=ALU.add).then_inc(x1_ready, 1)
                    return
                V.tensor_scalar(tmp[:], flat(mlp_banks(s)), b2_col[:, 0:1], None, ALU.add).then_inc(tmp_done, 1)
                dve.wait_ge(tmp_done, 2 * p + 1)
                V.scalar_tensor_tensor(out=tmp[:], in0=iota_t[:], scalar=seq_pair[:, bass.ds(p, 1)],
                                       in1=tmp[:], op0=ALU.is_lt, op1=ALU.mult).then_inc(tmp_done, 1)
                dve.wait_ge(tmp_done, 2 * p + 2)
                V.tensor_tensor(xt[:, s, :], xt[:, s, :], tmp[:], ALU.add).then_inc(x1_ready, 1)

            def step(i, last, masked):
                for s in range(NX):
                    over, slot = divmod(s + AHEAD, NX)
                    if not (last and over):
                        split_lo(i + over, slot, not isinstance(i, int) or i + over >= POOL_TURN)
                    add_mlp(i, s, masked)

            def stage1(masked):
                for s in range(AHEAD):
                    split_lo(0, s, False)
                for i in range(3):
                    step(i, False, masked)
                coefficients()
                for i in range(3, K_STEP):
                    step(i, False, masked)
                split_kernel()
                with dve.Fori(K_STEP, STEPS - 1) as i:
                    step(i, False, masked)
                step(STEPS - 1, True, masked)

            shortest = dve.value_load(seq_min_i[0:1, 0:1])
            before = chain[0]
            with dve.If(shortest < T):
                stage1(True)
            chain[0] = before
            with dve.Else():
                stage1(False)

            dve.wait_ge(x1_ready, PAIRS)
            V.tensor_scalar(mask, iota_t[:], len_f[:, 0:1], None, ALU.is_lt).then_inc(mask_ready, 1)
            dve.wait_ge(mask_ready, 1)

            def split_u(i, s):
                h = i * NX + s
                for q in range(2):
                    blocks = slice(q * (NB // 2), (q + 1) * (NB // 2))
                    dve.wait_ge(u_hi_done, 2 * h + q + 1)
                    V.scalar_tensor_tensor(out=u_lo[:, s % 2, blocks, :].rearrange("p k b -> p (k b)"),
                                           in0=turn_bank(q), scalar=SCALE,
                                           in1=u_hi[:, s % 2, blocks, :].rearrange("p k b -> p (k b)"),
                                           op0=ALU.mult, op1=ALU.subtract).then_inc(u_split, 1)

            def finish(h, s):
                dve.wait_ge(y_scaled, h + 1)
                dve.sem_inc(dve_passed, 1)
                V.copy_predicated(xt[:, s, :], mask.bitcast(I32), ys[:, s % 2, :]).then_inc(out_ready, 1)

            def step2(i, last):
                for s in range(NX):
                    if s < NX - 1:
                        split_u(i, s + 1)
                    elif not last:
                        split_u(i + 1, 0)
                    finish(i * NX + s, s)

            split_u(0, 0)
            with dve.Fori(0, CSTEPS - 1) as i:
                step2(i, False)
            step2(CSTEPS - 1, True)

        @block.tensor
        def _(pe):
            M = nc.tensor.matmul
            pe.wait_ge(s_small, 80)
            pe.wait_ge(s_onehot, 1)
            M(psum[:, 7, 0:B], bs_sb[:], onehot[:], start=True, stop=True).then_inc(s_biasmm, 1)
            pe.wait_ge(s_par2, 1)
            pe.wait_ge(s_ident, 1)
            for k in range(4):
                ins = nc.tensor.transpose(psum[:, 6, k * H:(k + 1) * H], par2[:, k].rearrange("h a n -> h (a n)"),
                                          ident[0:H, 0:H])
            ins.then_inc(s_parT, 1)

            w_flat = w_tab[:].rearrange("p s h d -> p (s h d)")

            def offsets(i):
                _, values = nc.values_load_multi_w_load_instructions(
                    w_offset[0:1, bass.ds(i * 2 * NX, 2 * NX)], engines=[mybir.EngineType.PE],
                    min_val=0, max_val=(S - 1) * 2 * HID,
                    skip_runtime_bounds_check_because="w_offset is clamped to the table where it is made")
                return values

            def hidden(i, s, j, first, at):
                p = i * NX + s
                pe.wait_ge(x_split, 2 * p + j + 1)
                if not (first and s == 0):
                    pe.wait_ge(gelu_done, 2 * (p - 1) + j + 1)
                for bank in range(2):
                    cols = slice(bank * HALF, (bank + 1) * HALF)
                    for half in range(2):
                        ins = M(hid_banks(j)[:, bank, :], w_flat[:, bass.ds(at[2 * s + j] + half * HID, HID)],
                                xs[:, s % NS, j, cols], start=(half == 0), stop=(half == 1))
                ins.then_inc(h_ready, 1)

            def output(p, s, first):
                pe.wait_ge(gelu_done, 2 * p + 2)
                if not first:
                    pe.wait_ge(x1_ready, p - 1)
                for bank in range(2):
                    for j in range(2):
                        ins = M(mlp_banks(s)[j * H:(j + 1) * H, bank, :], w2_sb[:],
                                hid[:, s % 2, j, bank * HALF:(bank + 1) * HALF], start=True, stop=True)
                ins.then_inc(o_ready, 1)

            def step(i, first, behind_kernel):
                at = offsets(i)
                for s in range(NX):
                    for j in range(2):
                        hidden(i, s, j, first, at)
                    if s == 1 and behind_kernel:
                        pe.wait_ge(s_ksplit, 2)
                    if not (s == 0 and (first or behind_kernel)):
                        output(i * NX + s - 1, (s - 1) % NX, first and s < 3)

            pe.wait_ge(s_offset, 1)
            pe.wait_ge(s_wsplit, 1)
            step(0, True, False)
            with pe.Fori(1, K_STEP) as i:
                step(i, False, False)
            output(K_STEP * NX - 1, NX - 1, False)

            pe.wait_ge(s_gmat, 1)
            pe.wait_ge(x1_ready, K_STEP * NX)
            for h in range(H):
                ins = M(kpsum[:, h, :], gmat[:, h, :], emat[:, h, :], start=True, stop=True)
            ins.then_inc(s_kmm, 1)

            step(K_STEP, False, True)
            with pe.Fori(K_STEP + 1, STEPS) as i:
                step(i, False, False)
            output(PAIRS - 1, NX - 1, False)

            def turn(i, s, first):
                h = i * NX + s
                pe.wait_ge(c_loaded[s], 16 * (i + 1))
                for q in range(2):
                    if not (first and s == 0):
                        pe.wait_ge(u_split, 2 * (h - 1) + q + 1)
                    for b in range(NB // 2):
                        k = q * (NB // 2) + b
                        ins = nc.tensor.transpose(turn_bank(q)[:, b * P:(b + 1) * P], xt[:, s, k * P:(k + 1) * P], ident[:])
                    ins.then_inc(turned, 1)

            def conv(i, s, first):
                h = i * NX + s
                pe.wait_ge(t_loaded[s % NT], 16 * (i * (NX // NT) + s // NT + 1))
                pe.wait_ge(u_split, 2 * h + 2)
                if not (first and s < 2):
                    pe.wait_ge(y_scaled, h - 1)
                y = y_banks(s)
                for k in range(NB):
                    for u, half in ((u_hi, 0), (u_hi, 1), (u_lo, 0)):
                        for bank in range(2):
                            begin, end = bank * HALF, min(T - k * P, (bank + 1) * HALF)
                            if begin >= end:
                                continue
                            ins = M(y[:, begin:end], u[:, s % 2, k, :], toep[:, s % NT, half, k * P + begin:k * P + end],
                                    start=(k == 0 and u is u_hi and half == 0),
                                    stop=(k == NB - 1 - bank * NB // 2 and u is u_lo))
                ins.then_inc(conv_done, 1)

            def step2(i, first, last):
                for s in range(NX):
                    if s < NX - 1:
                        turn(i, s + 1, first)
                    elif not last:
                        turn(i + 1, 0, False)
                    conv(i, s, first)

            pe.wait_ge(x1_ready, PAIRS)
            pe.wait_ge(mask_ready, 1)
            turn(0, 0, True)
            step2(0, True, False)
            with pe.Fori(1, CSTEPS - 1) as i:
                step2(i, False, False)
            step2(CSTEPS - 1, False, True)


_INS = ['x', 'itok_B_0_7', 'itok_B_2182_4065', 'itok_B_78_3631', '_lenS', 'L0_cond_W_sess', 'L0_cond_b_sess',
        'L0_cond_W2', 'L0_cond_b2', 'L1_cond_log_dt', 'L1_cond_C', 'L1_cond_log_A_real', 'L1_cond_A_imag', 'L1_cond_D']
_OUTS = [((128, 64, 1024), 'float32')]


def kernel(**inputs):
    import numpy as _np
    import concourse.bacc as _bacc
    from concourse import mybir as _mybir
    from concourse.bass_utils import run_bass_kernel_spmd as _run

    nc = _bacc.Bacc("TRN2", target_bir_lowering=False, num_devices=1)
    arrays, args = {}, []
    for name in _INS:
        a = _np.ascontiguousarray(inputs[name])
        arrays[f"in_{name}_dram"] = a
        args.append(nc.dram_tensor(f"in_{name}_dram", a.shape, _mybir.dt.from_np(a.dtype), kind="ExternalInput").ap())
    for i, (shape, dtype) in enumerate(_OUTS):
        dt = _mybir.dt.from_np(_np.dtype(dtype))
        args.append(nc.dram_tensor(f"out_{i}_dram", shape, dt, kind="ExternalOutput").ap())
    build_cond_residual(nc, *args)
    r = _run(nc, [arrays], core_ids=[0])
    got = tuple(r.results[0][f"out_{i}_dram"] for i in range(len(_OUTS)))
    return got[0]
```

```python
import math
from contextlib import ExitStack

import concourse.bass as bass
from concourse import mybir

ALU = mybir.AluOpType
ACT = mybir.ActivationFunctionType
AX_X = mybir.AxisListType.X
F32 = mybir.dt.float32
F16 = mybir.dt.float16
I32 = mybir.dt.int32

P = 128
SCALE = 256.0
UNSCALE = 1.0 / (SCALE * SCALE)
MAGIC = 12582912.0
TWO_PI_PARTS = (6.28125, 0.0019353071795864769)
LN2_PARTS = (0.693359375, -2.12194440054691e-04)
PI_BELOW = 3.1415925


def build_cond_residual(
    nc: bass.Bass,
    x: bass.AP,
    session_ids: bass.AP,
    seq_lens: bass.AP,
    conv_lens: bass.AP,
    channel_counts: bass.AP,
    W_sess: bass.AP,
    b_sess: bass.AP,
    W2: bass.AP,
    b2: bass.AP,
    log_dt: bass.AP,
    C: bass.AP,
    log_A_real: bass.AP,
    A_imag: bass.AP,
    D: bass.AP,
    out: bass.AP,
):
    B, H, T = x.shape
    S, _, HID = W_sess.shape
    N = A_imag.shape[1]
    assert B == P and HID == P and 2 * H == P and 2 * N == P
    HALF = T // 2
    PAIRS = B // 2
    NB = T // P
    TA = TB = 32
    LOW, HIGH = 4, 8
    TIMES = 2 * (LOW + HIGH)
    assert TA * TB == T and HALF == 512 and LOW * HIGH == TA == TB
    Q = T // 4
    K_COLS = T - Q
    TW = 2 * K_COLS
    KROW = TW + P

    x1_dram = nc.dram_tensor("x1_scratch", (H, B, T), F32).ap()
    k_dram = nc.dram_tensor("k_bounce", (H, T), F32).ap()
    k_scratch = nc.dram_tensor("k_halves", (2, H, KROW), F16)
    halves_dram = k_scratch.ap()

    NX = 8
    NS = 4
    NT = 4
    AHEAD = 2

    with ExitStack() as ctx:
        def sb(name, shape, dt):
            return ctx.enter_context(nc.sbuf_tensor(name, shape, dt))

        def sem(name):
            return ctx.enter_context(nc.semaphore(name))

        psum = ctx.enter_context(nc.psum_tensor("psum", [P, 8, HALF], F32))

        ident = sb("ident", [P, P], F32)
        iota_t = sb("iota_t", [P, T], F32)
        chan_of_part = sb("chan_of_part", [P, 1], F32)
        part_index = sb("part_index", [P, 1], F32)
        sid_i = sb("sid_i", [P, B], I32)
        cnt_i = sb("cnt_i", [P, B], I32)
        seq_i = sb("seq_i", [P, B], I32)
        len_i = sb("len_i", [P, 1], I32)
        sid_f = sb("sid_f", [P, B], F32)
        cnt_f = sb("cnt_f", [P, B], F32)
        seq_f = sb("seq_f", [P, B], F32)
        seq_pair = sb("seq_pair", [P, PAIRS], F32)
        len_f = sb("len_f", [P, 1], F32)
        live = sb("live", [P, B], F32)
        w_offset_f = sb("w_offset_f", [1, B], F32)
        w_offset = sb("w_offset", [1, B], I32)
        channel_scale = sb("channel_scale", [P, PAIRS], F32)
        scale_now = sb("scale_now", [P, NX], F32)
        onehot = sb("onehot", [S, B], F32)
        bs_sb = sb("bs_sb", [S, HID], F32)
        bias_all = sb("bias_all", [P, B], F32)
        w2_sb = sb("w2_sb", [P, H], F32)
        b2_col = sb("b2_col", [P, 1], F32)
        seq_min = sb("seq_min", [1, 2], F32)
        seq_min_i = sb("seq_min_i", [1, 1], I32)
        ws_raw = sb("ws_raw", [P, S, HID], F32)
        w_tab = sb("w_tab", [P, S, 2, HID], F16)
        zeros16 = sb("zeros16", [H, P], F16)
        warm = sb("warm", [H, 1], F32)

        par = sb("par", [H, 4 * N], F32)
        par2 = sb("par2", [H, 4, 2, N], F32)
        parT = sb("parT", [P, 4, H], F32)
        ex = sb("ex", [P, 2, H], F32)
        small = sb("small", [P, 28, H], F32)
        expo = sb("expo", [P, 4, H], F32)
        times = sb("times", [P, TIMES], F32)
        tab_im = sb("tab_im", [P, H, TIMES], F32)
        tab_re = sb("tab_re", [P, H, TIMES], F32)
        tab_c = sb("tab_c", [P, H, TIMES], F32)
        tab_k = sb("tab_k", [P, H, TIMES], F32)
        low = sb("low", [P, 4, H, LOW], F32)
        gmat = sb("gmat", [P, H, TA], F32)
        emat = sb("emat", [P, H, TB], F32)
        outer = sb("outer", [P, H, TA], F32)
        is_top = sb("is_top", [P, 1], F32)
        is_bottom = sb("is_bottom", [P, 1], F32)
        k_raw = sb("k_raw", [TA, H, TB], F32)
        k_early = sb("k_early", [H, K_COLS], F32)
        k_rows = sb("k_rows", [H, 2, K_COLS], F32)
        k_hi = sb("k_hi", [H, 2, K_COLS], F16)
        k_lo = sb("k_lo", [H, 2, K_COLS], F16)
        d_col = sb("d_col", [H, 1], F32)

        xt = sb("xt", [P, NX, T], F32)
        xs = sb("xs", [P, NS, 2, T], F16)
        hid = sb("hid", [P, 2, 2, T], F32)
        tmp = sb("tmp", [P, T], F32)

        toep = sb("toep", [P, NT, 2, TW], F16)
        u_hi = xs[:, 0, :, :].rearrange("p s (k b) -> p s k b", b=P)
        u_lo = xs[:, 1, :, :].rearrange("p s (k b) -> p s k b", b=P)
        v_hi = xs[:, 2, :, 0:Q]
        v_lo = xs[:, 3, :, 0:Q]
        v32 = hid[:, 1, :, 0:Q]
        ys = hid[:, 0, :, :]

        s_ids = sem("s_ids")
        s_par = sem("s_par")
        s_wraw = sem("s_wraw")
        s_small = sem("s_small")
        s_bs = sem("s_bs")
        s_iota = sem("s_iota")
        s_ident0 = sem("s_ident0")
        s_ident = sem("s_ident")
        s_chain = sem("s_chain")
        s_onehot = sem("s_onehot")
        s_biasmm = sem("s_biasmm")
        s_bias = sem("s_bias")
        s_zeros = sem("s_zeros")
        s_offset = sem("s_offset")
        s_scale = sem("s_scale")
        s_wsplit = sem("s_wsplit")
        s_par2 = sem("s_par2")
        s_parT = sem("s_parT")
        s_tables = sem("s_tables")
        s_abs2 = sem("s_abs2")
        s_re = sem("s_re")
        s_inv = sem("s_inv")
        s_pool = sem("s_pool")
        s_parC = sem("s_parC")
        s_trig = sem("s_trig")
        s_gmat = sem("s_gmat")
        s_kmm = sem("s_kmm")
        s_kraw = sem("s_kraw")
        s_kbounce = sem("s_kbounce")
        s_krow = sem("s_krow")
        s_ksplit = sem("s_ksplit")
        s_kstored = sem("s_kstored")

        x_loaded = [sem(f"x_loaded{n}") for n in range(NX)]
        x1_stored = [sem(f"x1_stored{n}") for n in range(NX)]
        scale_copied = sem("scale_copied")
        hi_by_act = [sem(f"hi_by_act{j}") for j in range(2)]
        hi_by_pool = sem("hi_by_pool")
        hi_by_dve = sem("hi_by_dve")
        x_split = sem("x_split")
        h_ready = sem("h_ready")
        gelu_done = sem("gelu_done")
        o_ready = sem("o_ready")
        x1_ready = sem("x1_ready")
        t_loaded = [sem(f"t_loaded{n}") for n in range(NT)]
        c_loaded = [sem(f"c_loaded{n}") for n in range(NX)]
        out_stored = [sem(f"out_stored{n}") for n in range(NX)]
        turned = sem("turned")
        u_hi_done = sem("u_hi_done")
        u_split = sem("u_split")
        conv_done = sem("conv_done")
        y_scaled = sem("y_scaled")
        out_ready = sem("out_ready")
        mask_ready = sem("mask_ready")
        u1_copied = sem("u1_copied")
        v_made = sem("v_made")
        v_hi_done = sem("v_hi_done")
        v_split = sem("v_split")
        combined = sem("combined")
        act_passed = sem("act_passed")
        pool_passed = sem("pool_passed")
        dve_passed = sem("dve_passed")
        tmp_done = sem("tmp_done")

        def hid_banks(j):
            return psum[:, 2 * j:2 * j + 2, :]

        def mlp_banks(s):
            return psum[:, 4 + 2 * (s % 2):6 + 2 * (s % 2), :]

        def flat(banks):
            return banks.rearrange("p a n -> p (a n)")

        def turn_bank(q):
            return psum[:, q, :]

        def y_banks(h):
            return psum[:, 2 + 2 * (h % 2):4 + 2 * (h % 2), :].rearrange("p a n -> p (a n)")

        def v_bank(h):
            return psum[:, 6 + h % 2, 0:Q]

        mask = iota_t[:]

        small_col = {}

        def sm(name):
            if name not in small_col:
                small_col[name] = len(small_col)
            return small[:, small_col[name], :]

        kpsum = psum[0:TA, 4:8, :].rearrange("p a n -> p (a n)").rearrange("p (h b) -> p h b", b=TB)


        STEPS = PAIRS // NX
        K_STEP = 4
        RECIPROCAL_STEP = 1
        POOL_TURN = 3
        DVE_SLOTS = (1, 4, 7)
        SPLIT_STEP = 5
        POOL_PAIR = POOL_TURN * NX
        CSTEPS = H // NX

        def by_dve(i, s):
            return isinstance(i, int) and i < POOL_TURN and s in DVE_SLOTS

        def second_rows_split(i, s, dve):
            return sum(by_dve(p // NX, p % NX) == dve for p in range(i * NX + s + 1))

        block = ctx.enter_context(nc.Block())

        @block.sync
        def _(sp):
            for ap, src in ((sid_i, session_ids), (cnt_i, channel_counts), (seq_i, seq_lens)):
                sp.dma_start(ap[:], src.partition_broadcast(P)).then_inc(s_ids, 16)
            sp.dma_start(len_i[:], conv_lens.rearrange("(b a) -> b a", a=1)).then_inc(s_ids, 16)
            def load_x(p, slot):
                sp.dma_start(xt[:, slot, :], x[bass.ds(2 * p, 2)].rearrange("b c t -> (b c) t")).then_inc(x_loaded[slot], 16)

            def store_x1(p, slot):
                for j in range(2):
                    sp.dma_start(x1_dram[:, bass.ds(2 * p + j, 1), :].rearrange("c b t -> (c b) t"),
                                 xt[j * H:(j + 1) * H, slot, :]).then_inc(x1_stored[slot], 16)

            def stage1_step(i, first, last, midway=None):
                for s in range(NX):
                    if midway and s == 2:
                        midway()
                    p = i * NX + s
                    sp.wait_ge(x1_ready, p + 1)
                    store_x1(p, s)
                    if not (last and s > 0):
                        nxt = (s + NX - 1) % NX
                        if not (first and s == 0):
                            sp.wait_ge(x1_stored[nxt], 32 * (i + (1 if s > 0 else 0)))
                            load_x(p + NX - 1, nxt)
                    if last and 0 < s <= NT:
                        load_toeplitz(s - 1, s - 1)

            def turn_kernel():
                sp.wait_ge(s_kraw, 2)
                sp.dma_start(k_dram.rearrange("h (a b) -> a h b", b=TB), k_raw[:]).then_inc(s_kbounce, 16)
                sp.wait_ge(s_kbounce, 16)
                sp.dma_start(k_early[:], k_dram[:, 0:K_COLS]).then_inc(s_krow, 16)
                sp.dma_start(k_rows[:, 1, :], k_dram[:, Q:T]).then_inc(s_krow, 16)

            def store_kernel():
                sp.wait_ge(s_zeros, 1)
                sp.wait_ge(s_ksplit, 2)
                for half, src in enumerate((k_hi, k_lo)):
                    sp.dma_start(halves_dram[half, :, 0:TW], src[:].rearrange("h a n -> h (a n)")).then_inc(s_kstored, 16)
                    sp.dma_start(halves_dram[half, :, TW:KROW], zeros16[:]).then_inc(s_kstored, 16)

            def load_toeplitz(h, slot):
                row = halves_dram[:, bass.ds(h, 1), :]
                sp.dma_start(toep[:, slot % NT, :, :], bass.AP(k_scratch, row.offset, [[1, P], [H * KROW, 2], [1, TW]])
                             ).then_inc(t_loaded[slot % NT], 16)

            load_x(0, 0)
            for j in range(2):
                sp.dma_start(ws_raw[j * H:(j + 1) * H, :, :], W_sess.rearrange("s c d -> c s d")).then_inc(s_wraw, 16)
            load_x(1, 1)
            sp.dma_start(w2_sb[:], W2).then_inc(s_small, 16)
            for j in range(2):
                sp.dma_start(b2_col[j * H:(j + 1) * H, :], b2.rearrange("(s a) -> s a", a=1)).then_inc(s_small, 16)
            sp.dma_start(d_col[:], D.rearrange("(s a) -> s a", a=1)).then_inc(s_small, 16)
            for s in range(2, NX):
                load_x(s, s)
            stage1_step(0, True, False)
            with sp.Fori(1, K_STEP) as i:
                stage1_step(i, False, False)
            stage1_step(K_STEP, False, False, midway=turn_kernel)
            for i in range(K_STEP + 1, SPLIT_STEP + 1):
                stage1_step(i, False, False)
            store_kernel()
            for i in range(SPLIT_STEP + 1, STEPS - 1):
                stage1_step(i, False, False)
            sp.wait_ge(s_kstored, 64)
            stage1_step(STEPS - 1, False, True)

            def load_channel(h, slot):
                sp.dma_start(xt[:, slot, :], x1_dram[bass.ds(h, 1)].rearrange("a b t -> (a b) t")).then_inc(c_loaded[slot], 16)

            def store_out(h, slot):
                sp.dma_start(out[:, bass.ds(h, 1), :].rearrange("b a t -> (b a) t"), xt[:, slot, :]).then_inc(out_stored[slot], 16)

            def stage2_step(i, first, last):
                for s in range(NX):
                    h = i * NX + s
                    sp.wait_ge(out_ready, h + 1)
                    store_out(h, s)
                    if not (last and s > 0) and not (first and s == 0):
                        nxt = (s + NX - 1) % NX
                        sp.wait_ge(out_stored[nxt], 16 * (i + (1 if s > 0 else 0)))
                        load_channel(h + NX - 1, nxt)
                    if not (last and s + NT >= NX):
                        load_toeplitz(h + NT, s)

            for s in range(NX):
                sp.wait_ge(x1_stored[s], 32 * STEPS)
            for s in range(NX):
                load_channel(s, s)
            stage2_step(0, True, False)
            with sp.Fori(1, CSTEPS - 1) as i:
                stage2_step(i, False, False)
            stage2_step(CSTEPS - 1, False, True)
            for s in range(NX):
                sp.wait_ge(out_stored[s], 16 * CSTEPS)

        @block.gpsimd
        def _(pool):
            nc.gpsimd.iota(iota_t[:], pattern=[[1, T]], base=0, channel_multiplier=0,
                           allow_small_or_imprecise_dtypes=True).then_inc(s_iota, 1)
            at = 0
            for unit in (1, TB):
                for step_, n in ((unit, LOW), (unit * LOW, HIGH)):
                    nc.gpsimd.iota(times[:, at:at + n], pattern=[[-step_, n]], base=step_ * (n - 1), channel_multiplier=0,
                                   allow_small_or_imprecise_dtypes=True).then_inc(s_iota, 1)
                    at += n
            nc.gpsimd.iota(part_index[:], pattern=[[0, 1]], base=0, channel_multiplier=1,
                           allow_small_or_imprecise_dtypes=True).then_inc(s_iota, 1)
            nc.gpsimd.memset(ident[:], 0.0).then_inc(s_ident0, 1)
            pool.wait_ge(s_ident0, 1)
            nc.gpsimd.affine_select(out=ident[:], in_=ident[:], compare_op=ALU.not_equal, fill=1.0, base=0,
                                    pattern=[[-1, P]], channel_multiplier=1).then_inc(s_ident, 1)

            done = [0]

            def link(ins):
                done[0] += 1
                ins.then_inc(s_pool, 1)
                pool.wait_ge(s_pool, done[0])

            mul = lambda o, a, b: nc.gpsimd.tensor_tensor(o, a, b, ALU.mult)
            add = lambda o, a, b: nc.gpsimd.tensor_tensor(o, a, b, ALU.add)
            sub = lambda o, a, b: nc.gpsimd.tensor_tensor(o, a, b, ALU.subtract)
            line = lambda o, a, m, c: nc.gpsimd.tensor_scalar(o, a, m, c, ALU.mult, ALU.add)
            shifted = lambda o, a, c, m: nc.gpsimd.tensor_scalar(o, a, c, m, ALU.add, ALU.mult)
            scaled = lambda o, a, m: nc.gpsimd.tensor_scalar(o, a, m, 1.0, ALU.mult, ALU.mult)

            pool.wait_ge(s_parC, 1)
            pool.wait_ge(s_par, 64)
            link(scaled(ex[:, 1, :], parT[:, 0, :], 1.0))
            v = ex[:]
            k = expo[:, 0:2, :]
            acc = expo[:, 2:4, :]
            link(line(k, v, 1.0 / math.log(2.0), MAGIC))
            link(shifted(k, k, -MAGIC, 1.0))
            for part in LN2_PARTS:
                link(scaled(acc, k, -part))
                link(add(v, v, acc))
            link(line(acc, v, 1.0 / math.factorial(7), 1.0 / math.factorial(6)))
            for n in range(5, -1, -1):
                link(mul(acc, acc, v))
                link(shifted(acc, acc, 1.0 / math.factorial(n), 1.0))
            link(shifted(v.bitcast(I32), k, 127.0, float(1 << 23)))
            link(mul(ex[:], acc, v))
            dt, rate = ex[:, 0, :], ex[:, 1, :]
            a_im, c_re, c_im = parT[:, 1, :], parT[:, 2, :], parT[:, 3, :]
            mul(sm("im"), a_im, dt)
            scaled(sm("a_re"), rate, -1.0)
            mul(sm("aim2"), a_im, a_im)
            link(mul(sm("abs2"), rate, rate))
            add(sm("abs2"), sm("abs2"), sm("aim2")).then_inc(s_abs2, 1)
            mul(sm("re"), sm("a_re"), dt).then_inc(s_re, 1)
            pool.wait_ge(s_re, 1)

            def over_times(v):
                return (v.unsqueeze(2).to_broadcast([P, H, TIMES]), times[:].unsqueeze(1).to_broadcast([P, H, TIMES]))

            mul(tab_re[:], *over_times(sm("re")))
            link(mul(tab_im[:], *over_times(sm("im"))))
            link(line(tab_k[:], tab_im[:], 1.0 / (2.0 * math.pi), MAGIC))
            link(nc.gpsimd.tensor_scalar(tab_k[:], tab_k[:], -MAGIC, -TWO_PI_PARTS[0], ALU.add, ALU.mult))
            link(add(tab_im[:], tab_im[:], tab_k[:]))
            link(nc.gpsimd.tensor_scalar(tab_k[:], tab_k[:], TWO_PI_PARTS[1] / TWO_PI_PARTS[0], 1.0, ALU.mult, ALU.mult))
            link(add(tab_im[:], tab_im[:], tab_k[:]))
            nc.gpsimd.tensor_scalar(tab_im[:], tab_im[:], PI_BELOW, -PI_BELOW, ALU.min, ALU.max).then_inc(s_tables, 1)

            pool.wait_ge(s_trig, 6)
            link(mul(tab_c[:], tab_c[:], tab_c[:]))
            mul(tab_im[:], tab_im[:], tab_re[:])
            link(line(tab_c[:], tab_c[:], -2.0, 1.0))
            link(mul(tab_c[:], tab_c[:], tab_re[:]))
            b_low, b_high, a_low, a_high = (slice(0, LOW), slice(LOW, LOW + HIGH), slice(LOW + HIGH, 2 * LOW + HIGH),
                                            slice(2 * LOW + HIGH, TIMES))
            u, v, w, z = (low[:, k] for k in range(4))

            def over_high(dst, high):
                shape = [P, H, HIGH, LOW]
                spread_low = lambda t: t.unsqueeze(2).to_broadcast(shape)
                spread_high = lambda t: t[:, :, high].unsqueeze(3).to_broadcast(shape)
                split = lambda t: t.rearrange("p h (x y) -> p h x y", y=LOW)
                mul(split(dst), spread_low(u), spread_high(tab_c))
                link(mul(split(outer[:]), spread_low(v), spread_high(tab_im)))
                return add(dst, dst, outer[:])

            scaled(u, tab_c[:, :, b_low], is_top[:, 0:1])
            scaled(w, tab_im[:, :, b_low], is_bottom[:, 0:1])
            scaled(v, tab_c[:, :, b_low], is_bottom[:, 0:1])
            link(scaled(z, tab_im[:, :, b_low], is_top[:, 0:1]))
            add(u, u, w)
            link(sub(v, v, z))
            link(over_high(emat[:], b_high))
            pool.wait_ge(s_inv, 1)
            mul(sm("em1"), sm("inv_t"), sm("t_step"))
            link(mul(sm("sin2"), sm("sin_half"), sm("sin_half")))
            line(sm("cos"), sm("sin2"), -2.0, 1.0)
            link(line(sm("exp"), sm("em1"), 2.0, 1.0))
            mul(sm("er"), sm("em1"), sm("cos"))
            link(mul(sm("ei"), sm("exp"), sm("sin")))
            sub(sm("er"), sm("er"), sm("sin2"))
            link(scaled(sm("ei"), sm("ei"), 0.5))
            scaled(sm("inv"), sm("inv"), 4.0)
            mul(sm("zr"), sm("er"), sm("a_re"))
            mul(sm("zr2"), sm("ei"), a_im)
            mul(sm("zi"), sm("ei"), sm("a_re"))
            link(mul(sm("zi2"), sm("er"), a_im))
            add(sm("zr"), sm("zr"), sm("zr2"))
            link(sub(sm("zi"), sm("zi"), sm("zi2")))
            mul(sm("zr"), sm("zr"), sm("inv"))
            link(mul(sm("zi"), sm("zi"), sm("inv")))
            mul(sm("er"), c_re, sm("zr"))
            mul(sm("zr2"), c_im, sm("zi"))
            mul(sm("ei"), c_re, sm("zi"))
            link(mul(sm("zi2"), c_im, sm("zr")))
            sub(sm("er"), sm("er"), sm("zr2"))
            link(add(sm("ei"), sm("ei"), sm("zi2")))
            negated = lambda o, a, m: nc.gpsimd.tensor_scalar(o, a, m, -1.0, ALU.mult, ALU.mult)
            scaled(sm("p_top"), sm("er"), is_top[:, 0:1])
            negated(sm("q_top"), sm("ei"), is_top[:, 0:1])
            negated(sm("gp"), sm("ei"), is_bottom[:, 0:1])
            link(negated(sm("gq"), sm("er"), is_bottom[:, 0:1]))
            add(sm("gp"), sm("gp"), sm("p_top"))
            link(add(sm("gq"), sm("gq"), sm("q_top")))
            per_mode = lambda t: sm(t).unsqueeze(2).to_broadcast([P, H, LOW])
            mul(u, tab_c[:, :, a_low], per_mode("gp"))
            mul(w, tab_im[:, :, a_low], per_mode("gq"))
            mul(v, tab_c[:, :, a_low], per_mode("gq"))
            link(mul(z, tab_im[:, :, a_low], per_mode("gp")))
            add(u, u, w)
            link(sub(v, v, z))
            over_high(gmat[:], a_high).then_inc(s_gmat, 1)
            pool.wait_ge(s_gmat, 1)

            def copy_scales(i):
                nc.gpsimd.tensor_copy(scale_now[:], channel_scale[:, bass.ds(i * NX, NX)]).then_inc(scale_copied, 1)

            def split_hi(i, s):
                p = i * NX + s
                pool.wait_ge(x_loaded[s], 16 * (i + 1))
                pool.wait_ge(h_ready, 2 * (p - NS) + 2)
                if s == 0:
                    pool.wait_ge(scale_copied, i - POOL_TURN + 1)
                pool.sem_inc(pool_passed, 1)
                nc.gpsimd.tensor_scalar(xs[H:P, s % NS, 1, :], xt[H:P, s, :], scale_now[H:P, s:s + 1], 1.0,
                                        ALU.mult, ALU.mult).then_inc(hi_by_pool, 1)

            def step(i, first):
                if not first:
                    pool.wait_ge(hi_by_pool, NX * i - POOL_PAIR)
                copy_scales(i)
                for s in range(NX):
                    split_hi(i, s)

            step(POOL_TURN, True)
            for i in range(POOL_TURN + 1, SPLIT_STEP):
                step(i, False)

            pool.wait_ge(s_small, 64)
            pool.wait_ge(s_krow, 32)
            last = k_rows[:, 1, K_COLS - 1:K_COLS]
            line(d_col[:], d_col[:], 1.0, 1.0)
            link(add(k_rows[:, 0, :], k_rows[:, 1, :], k_early[:]))
            link(add(last, last, d_col[:]))
            scaled(k_hi[:].rearrange("h a n -> h (a n)"), k_rows[:].rearrange("h a n -> h (a n)"), SCALE).then_inc(s_ksplit, 1)

            with pool.Fori(SPLIT_STEP, STEPS) as i:
                step(i, False)

        @block.scalar
        def _(act):
            act.dma_start(bs_sb[:], b_sess).then_inc(s_bs, 16)
            for ap, src in ((par[:, 0:N], log_A_real), (par[:, N:2 * N], A_imag),
                            (par[:, 2 * N:4 * N], C.rearrange("h n z -> h (n z)")), (ex[:, 0, :], log_dt.partition_broadcast(P))):
                act.dma_start(ap, src).then_inc(s_par, 16)
            def split_hi(i, s, j, first):
                p = i * NX + s
                q = slice(j * H, (j + 1) * H)
                act.wait_ge(x_loaded[s], 16 * (i + 1))
                if not (first and s < NS):
                    act.wait_ge(h_ready, 2 * (p - NS) + 2)
                act.sem_inc(act_passed, 1)
                nc.scalar.activation(xs[q, s % NS, j, :], xt[q, s, :], ACT.Copy,
                                     scale=channel_scale[q, bass.ds(p, 1)]).then_inc(hi_by_act[j], 1)

            def evacuate_kernel():
                for half in range(2):
                    act.wait_ge(s_kmm, half + 1)
                    channels = slice(half * H // 2, (half + 1) * H // 2)
                    nc.scalar.activation(k_raw[:, channels, :], kpsum[:, channels, :], ACT.Copy).then_inc(s_kraw, 1)

            def step(i, first, last, with_kernel=False):
                for s in range(NX):
                    p = i * NX + s
                    if with_kernel and s == 1:
                        evacuate_kernel()
                    for j in range(2):
                        act.wait_ge(h_ready, 2 * p + j + 1)
                        if j == 0 and not (first and s < 2):
                            act.wait_ge(o_ready, p - 1)
                        act.sem_inc(act_passed, 1)
                        nc.scalar.activation(hid[:, s % 2, j, :], flat(hid_banks(j)), ACT.Gelu,
                                             bias=bias_all[:, bass.ds(2 * p + j, 1)],
                                             scale=UNSCALE).then_inc(gelu_done, 1)
                        over, slot = divmod(s + AHEAD + 1, NX)
                        static = isinstance(i, int)
                        by_act = j == 0 or static and p + AHEAD + 1 < POOL_PAIR and not by_dve(i + over, slot)
                        if not (last and over) and by_act:
                            split_hi(i + over, slot, j, first and not over)

            act.wait_ge(s_zeros, 1)
            nc.scalar.activation(warm[:], zeros16[:, 0:1], ACT.Gelu)
            act.wait_ge(s_scale, 1)
            for s in range(AHEAD + 1):
                for j in range(1 if by_dve(0, s) else 2):
                    split_hi(0, s, j, True)
            act.wait_ge(s_bias, 1)
            step(0, True, False)
            act.wait_ge(s_re, 1)
            nc.scalar.activation(sm("t_step"), sm("re"), ACT.Tanh, scale=0.5).then_inc(s_trig, 1)
            act.wait_ge(s_tables, 1)
            nc.scalar.activation(tab_re[:], tab_re[:], ACT.Exp).then_inc(s_trig, 1)
            one = LOW - 2
            nc.scalar.activation(sm("sin_half"), tab_im[:, :, one], ACT.Sin, scale=0.5).then_inc(s_trig, 1)
            nc.scalar.activation(sm("sin"), tab_im[:, :, one], ACT.Sin).then_inc(s_trig, 1)
            nc.scalar.activation(tab_c[:], tab_im[:], ACT.Sin, scale=0.5).then_inc(s_trig, 1)
            act.wait_ge(s_trig, 5)
            nc.scalar.activation(tab_im[:], tab_im[:], ACT.Sin).then_inc(s_trig, 1)
            for i in range(1, POOL_TURN):
                step(i, False, False)
            for i in range(POOL_TURN, K_STEP):
                step(i, False, False)
            step(K_STEP, False, False, with_kernel=True)
            with act.Fori(K_STEP + 1, STEPS - 1) as i:
                step(i, False, False)
            step(STEPS - 1, False, True)

            def split_hi(i, s, first):
                h = i * NX + s
                for q in range(2):
                    act.wait_ge(turned, 2 * h + q + 1)
                    if q == 0 and not (first and s < 2):
                        act.wait_ge(conv_done, h - 1)
                    nc.scalar.activation(u_hi[:, s % 2, q * (NB // 2):(q + 1) * (NB // 2), :].rearrange("p k b -> p (k b)"),
                                         turn_bank(q), ACT.Copy, scale=SCALE).then_inc(u_hi_done, 1)

                    if q == 0:
                        nc.scalar.activation(v32[:, s % 2, :], turn_bank(0)[:, Q:2 * Q], ACT.Copy).then_inc(u1_copied, 1)
                act.wait_ge(v_made, h + 1)
                nc.scalar.activation(v_hi[:, s % 2, :], v32[:, s % 2, :], ACT.Copy, scale=SCALE).then_inc(v_hi_done, 1)

            def unscale(h, s, first):
                act.wait_ge(conv_done, h + 1)
                if not (first and s < 2):
                    act.wait_ge(out_ready, h - 1)
                y = y_banks(s)
                nc.scalar.activation(ys[:, s % 2, :], bass.AP(y.tensor, y.offset + T - 1, [y.ap[0], [-1, T]]), ACT.Copy,
                                     scale=UNSCALE).then_inc(y_scaled, 1)

            def step2(i, first, last):
                for s in range(NX):
                    over, slot = divmod(s + 2, NX)
                    if not (last and over):
                        split_hi(i + over, slot, first and not over)
                    unscale(i * NX + s, s, first)

            split_hi(0, 0, True)
            split_hi(0, 1, True)
            step2(0, True, False)
            with act.Fori(1, CSTEPS - 1) as i:
                step2(i, False, False)
            step2(CSTEPS - 1, False, True)

        @block.vector
        def _(dve):
            chain = [0]

            def link(ins):
                chain[0] += 1
                ins.then_inc(s_chain, 1)
                dve.wait_ge(s_chain, chain[0])

            V = nc.vector
            V.memset(zeros16[:], 0.0).then_inc(s_zeros, 1)

            dve.wait_ge(s_ids, 64)
            dve.wait_ge(s_iota, 6)
            V.tensor_copy(chan_of_part[0:H, :], part_index[0:H, :])
            V.tensor_scalar(chan_of_part[H:P, :], part_index[H:P, :], float(-H), None, ALU.add)
            V.tensor_copy(sid_f[:], sid_i[:])
            V.tensor_copy(len_f[:], len_i[:])
            V.tensor_copy(seq_f[:], seq_i[:])
            link(V.tensor_copy(cnt_f[:], cnt_i[:]))
            V.tensor_scalar(onehot[:], sid_f[0:S, :], part_index[0:S, 0:1], None, ALU.is_equal).then_inc(s_onehot, 1)
            V.tensor_scalar(w_offset_f[:], sid_f[0:1, :], float(S - 1), 0.0, ALU.min, ALU.max)
            link(V.tensor_scalar(live[:], cnt_f[:], chan_of_part[:, 0:1], SCALE, ALU.is_gt, ALU.mult))
            for j in range(2):
                q = slice(j * H, (j + 1) * H)
                ins = V.tensor_copy(channel_scale[q, :], live[q, :].rearrange("p (n j) -> p n j", j=2)[:, :, j])
            ins.then_inc(s_scale, 1)
            V.tensor_scalar(w_offset[:], w_offset_f[:], 2.0 * HID, None, ALU.mult).then_inc(s_offset, 1)
            for j in range(2):
                q = slice(j * H, (j + 1) * H)
                V.tensor_copy(seq_pair[q, :], seq_f[q, :].rearrange("p (n j) -> p n j", j=2)[:, :, j])
            link(V.tensor_reduce(seq_min[:, 0:1], seq_f[0:1, :], AX_X, ALU.min))
            link(V.tensor_copy(seq_min_i[:], seq_min[:, 0:1]))
            V.tensor_scalar(is_bottom[:], part_index[:], float(N), None, ALU.is_ge)
            V.tensor_scalar(is_top[:], part_index[:], float(N), None, ALU.is_lt)

            dve.wait_ge(s_par, 64)
            c_parts = par[:, 2 * N:4 * N].rearrange("h (n z) -> h n z", z=2)
            for k, v in enumerate((par[:, 0:N], par[:, N:2 * N], c_parts[:, :, 0], c_parts[:, :, 1])):
                ins = V.tensor_copy(par2[:, k], v.unsqueeze(1).to_broadcast([H, 2, N]))
            ins.then_inc(s_par2, 1)

            dve.wait_ge(s_wraw, 32)
            link(V.tensor_scalar(w_tab[:, :, 0, :], ws_raw[:], SCALE, None, ALU.mult))
            V.scalar_tensor_tensor(out=w_tab[:, :, 1, :], in0=ws_raw[:], scalar=SCALE, in1=w_tab[:, :, 0, :],
                                   op0=ALU.mult, op1=ALU.subtract).then_inc(s_wsplit, 1)
            dve.wait_ge(s_biasmm, 1)
            V.tensor_copy(bias_all[:], psum[:, 7, 0:B]).then_inc(s_bias, 1)
            dve.wait_ge(s_parT, 1)
            V.tensor_copy(parT[:], psum[:, 6, 0:4 * H].rearrange("p (k h) -> p k h", k=4)).then_inc(s_parC, 1)

            def reciprocals():
                dve.wait_ge(s_abs2, 1)
                dve.wait_ge(s_trig, 1)
                link(V.tensor_scalar(sm("one_minus_t"), sm("t_step"), -1.0, 1.0, ALU.mult, ALU.add))
                V.reciprocal(sm("inv"), sm("abs2"))
                V.reciprocal(sm("inv_t"), sm("one_minus_t")).then_inc(s_inv, 1)

            def split_kernel():
                dve.wait_ge(s_ksplit, 1)
                V.scalar_tensor_tensor(out=k_lo[:].rearrange("h a n -> h (a n)"), in0=k_rows[:].rearrange("h a n -> h (a n)"),
                                       scalar=SCALE, in1=k_hi[:].rearrange("h a n -> h (a n)"),
                                       op0=ALU.mult, op1=ALU.subtract).then_inc(s_ksplit, 1)

            def split_lo(i, s, by_pool):
                p = i * NX + s
                for j in range(2):
                    q = slice(j * H, (j + 1) * H)
                    other = slice((1 - j) * H, (2 - j) * H)
                    if j == 1 and by_pool:
                        dve.wait_ge(hi_by_pool, p - POOL_PAIR + 1)
                    elif j == 1 and by_dve(i, s):
                        if p >= NS:
                            dve.wait_ge(h_ready, 2 * (p - NS) + 2)
                        dve.wait_ge(x_loaded[s], 16 * (i + 1))
                        V.tensor_scalar(xs[q, s % NS, j, :], xt[q, s, :], channel_scale[q, bass.ds(p, 1)], None,
                                        ALU.mult).then_inc(hi_by_dve, 1)
                        dve.wait_ge(hi_by_dve, second_rows_split(i, s, True))
                    elif j == 1:
                        dve.wait_ge(hi_by_act[j], second_rows_split(i, s, False))
                    else:
                        dve.wait_ge(hi_by_act[j], p + 1)
                    V.scalar_tensor_tensor(out=xs[other, s % NS, j, :], in0=xt[q, s, :],
                                           scalar=channel_scale[q, bass.ds(p, 1)],
                                           in1=xs[q, s % NS, j, :], op0=ALU.mult, op1=ALU.subtract).then_inc(x_split, 1)

            def add_mlp(i, s, masked):
                p = i * NX + s
                dve.wait_ge(o_ready, p + 1)
                if not masked:
                    V.scalar_tensor_tensor(out=xt[:, s, :], in0=flat(mlp_banks(s)), scalar=b2_col[:, 0:1],
                                           in1=xt[:, s, :], op0=ALU.add, op1=ALU.add).then_inc(x1_ready, 1)
                    return
                if not (isinstance(p, int) and p == 0):
                    dve.wait_ge(x1_ready, p)
                dve.sem_inc(dve_passed, 1)
                V.tensor_scalar(tmp[:], flat(mlp_banks(s)), b2_col[:, 0:1], None, ALU.add).then_inc(tmp_done, 1)
                dve.wait_ge(tmp_done, 2 * p + 1)
                V.scalar_tensor_tensor(out=tmp[:], in0=iota_t[:], scalar=seq_pair[:, bass.ds(p, 1)],
                                       in1=tmp[:], op0=ALU.is_lt, op1=ALU.mult).then_inc(tmp_done, 1)
                dve.wait_ge(tmp_done, 2 * p + 2)
                V.tensor_tensor(xt[:, s, :], xt[:, s, :], tmp[:], ALU.add).then_inc(x1_ready, 1)

            def step(i, last, masked):
                for s in range(NX):
                    over, slot = divmod(s + AHEAD, NX)
                    if not (last and over):
                        split_lo(i + over, slot, not isinstance(i, int) or i + over >= POOL_TURN)
                    add_mlp(i, s, masked)

            def stage1(masked):
                dve.wait_ge(s_small, 64)
                for s in range(AHEAD):
                    split_lo(0, s, False)
                for i in range(RECIPROCAL_STEP):
                    step(i, False, masked)
                reciprocals()
                for i in range(RECIPROCAL_STEP, SPLIT_STEP):
                    step(i, False, masked)
                split_kernel()
                with dve.Fori(SPLIT_STEP, STEPS - 1) as i:
                    step(i, False, masked)
                step(STEPS - 1, True, masked)

            shortest = dve.value_load(seq_min_i[0:1, 0:1])
            before = chain[0]
            with dve.If(shortest < T):
                stage1(True)
            chain[0] = before
            with dve.Else():
                stage1(False)

            dve.wait_ge(x1_ready, PAIRS)
            V.tensor_scalar(mask, iota_t[:], len_f[:, 0:1], None, ALU.is_lt).then_inc(mask_ready, 1)
            dve.wait_ge(mask_ready, 1)

            def split_u(i, s):
                h = i * NX + s
                for q in range(2):
                    blocks = slice(q * (NB // 2), (q + 1) * (NB // 2))
                    if q == 0:
                        dve.wait_ge(u1_copied, h + 1)
                    else:
                        dve.wait_ge(u_hi_done, 2 * h + 2)
                    V.scalar_tensor_tensor(out=u_lo[:, s % 2, blocks, :].rearrange("p k b -> p (k b)"),
                                           in0=turn_bank(q), scalar=SCALE,
                                           in1=u_hi[:, s % 2, blocks, :].rearrange("p k b -> p (k b)"),
                                           op0=ALU.mult, op1=ALU.subtract).then_inc(u_split, 1)
                    if q == 0:
                        V.tensor_tensor(v32[:, s % 2, :], turn_bank(0)[:, 0:Q], v32[:, s % 2, :],
                                        ALU.subtract).then_inc(v_made, 1)
                dve.wait_ge(v_hi_done, h + 1)
                V.scalar_tensor_tensor(out=v_lo[:, s % 2, :], in0=v32[:, s % 2, :], scalar=SCALE, in1=v_hi[:, s % 2, :],
                                       op0=ALU.mult, op1=ALU.subtract).then_inc(v_split, 1)

            def finish(h, s):
                dve.wait_ge(y_scaled, h + 1)
                dve.sem_inc(dve_passed, 1)
                v = v_bank(s)
                backwards = bass.AP(v.tensor, v.offset + Q - 1, [v.ap[0], [-1, Q]])
                third, last = (ys[:, s % 2, n * Q:(n + 1) * Q] for n in (2, 3))
                V.scalar_tensor_tensor(out=third, in0=backwards, scalar=UNSCALE, in1=third, op0=ALU.mult, op1=ALU.add)
                V.scalar_tensor_tensor(out=last, in0=backwards, scalar=-UNSCALE, in1=last,
                                       op0=ALU.mult, op1=ALU.add).then_inc(combined, 1)
                dve.wait_ge(combined, h + 1)
                dve.sem_inc(dve_passed, 1)
                V.copy_predicated(xt[:, s, :], mask.bitcast(I32), ys[:, s % 2, :]).then_inc(out_ready, 1)

            def step2(i, last):
                for s in range(NX):
                    over, slot = divmod(s + 2, NX)
                    if not (last and over):
                        split_u(i + over, slot)
                    finish(i * NX + s, s)

            split_u(0, 0)
            split_u(0, 1)
            with dve.Fori(0, CSTEPS - 1) as i:
                step2(i, False)
            step2(CSTEPS - 1, True)

        @block.tensor
        def _(pe):
            M = nc.tensor.matmul
            pe.wait_ge(s_bs, 16)
            pe.wait_ge(s_onehot, 1)
            M(psum[:, 7, 0:B], bs_sb[:], onehot[:], start=True, stop=True).then_inc(s_biasmm, 1)
            pe.wait_ge(s_par2, 1)
            pe.wait_ge(s_ident, 1)
            for k in range(4):
                ins = nc.tensor.transpose(psum[:, 6, k * H:(k + 1) * H], par2[:, k].rearrange("h a n -> h (a n)"),
                                          ident[0:H, 0:H])
            ins.then_inc(s_parT, 1)

            w_flat = w_tab[:].rearrange("p s h d -> p (s h d)")

            def offsets(i):
                _, values = nc.values_load_multi_w_load_instructions(
                    w_offset[0:1, bass.ds(i * 2 * NX, 2 * NX)], engines=[mybir.EngineType.PE],
                    min_val=0, max_val=(S - 1) * 2 * HID,
                    skip_runtime_bounds_check_because="w_offset is clamped to the table where it is made")
                return values

            def hidden(i, s, j, first, at):
                p = i * NX + s
                pe.wait_ge(x_split, 2 * p + j + 1)
                if not (first and s == 0):
                    pe.wait_ge(gelu_done, 2 * (p - 1) + j + 1)
                for bank in range(2):
                    cols = slice(bank * HALF, (bank + 1) * HALF)
                    for half in range(2):
                        ins = M(hid_banks(j)[:, bank, :], w_flat[:, bass.ds(at[2 * s + j] + half * HID, HID)],
                                xs[:, s % NS, j, cols], start=(half == 0), stop=(half == 1))
                ins.then_inc(h_ready, 1)

            def output(p, s, first):
                pe.wait_ge(gelu_done, 2 * p + 2)
                if not first:
                    pe.wait_ge(x1_ready, p - 1)
                for bank in range(2):
                    for j in range(2):
                        ins = M(mlp_banks(s)[j * H:(j + 1) * H, bank, :], w2_sb[:],
                                hid[:, s % 2, j, bank * HALF:(bank + 1) * HALF], start=True, stop=True)
                ins.then_inc(o_ready, 1)

            def kernel_products():
                pe.wait_ge(s_gmat, 1)
                for half in range(2):
                    pe.wait_ge(x1_ready, K_STEP * NX - 1 + half)
                    for h in range(half * H // 2, (half + 1) * H // 2):
                        ins = M(kpsum[:, h, :], gmat[:, h, :], emat[:, h, :], start=True, stop=True)
                    ins.then_inc(s_kmm, 1)

            def step(i, first, with_kernel):
                at = offsets(i)
                for s in range(NX):
                    for j in range(2):
                        hidden(i, s, j, first, at)
                    if with_kernel and 1 <= s <= 2:
                        pe.wait_ge(s_kraw, s)
                    if not (first and s == 0):
                        output(i * NX + s - 1, (s - 1) % NX, first and s < 3)
                    if with_kernel and s == 0:
                        kernel_products()

            pe.wait_ge(s_offset, 1)
            pe.wait_ge(s_wsplit, 1)
            pe.wait_ge(s_small, 64)
            step(0, True, False)
            with pe.Fori(1, K_STEP) as i:
                step(i, False, False)
            step(K_STEP, False, True)
            with pe.Fori(K_STEP + 1, STEPS) as i:
                step(i, False, False)
            output(PAIRS - 1, NX - 1, False)

            def turn(i, s, first):
                h = i * NX + s
                pe.wait_ge(c_loaded[s], 16 * (i + 1))
                for q in range(2):
                    if not (first and s == 0):
                        if q == 0:
                            pe.wait_ge(v_made, h)
                        else:
                            pe.wait_ge(u_split, 2 * h)
                    for b in range(NB // 2):
                        k = q * (NB // 2) + b
                        ins = nc.tensor.transpose(turn_bank(q)[:, b * P:(b + 1) * P], xt[:, s, k * P:(k + 1) * P], ident[:])
                    ins.then_inc(turned, 1)

            def conv(i, s, first):
                h = i * NX + s
                pe.wait_ge(t_loaded[s % NT], 16 * (i * (NX // NT) + s // NT + 1))
                pe.wait_ge(u_split, 2 * h + 2)
                if not (first and s < 2):
                    pe.wait_ge(combined, h - 1)
                y = y_banks(s)
                half_blocks = NB // 2
                own = lambda half, begin, end: toep[:, s % NT, half, K_COLS + begin - Q:K_COLS + end - Q]
                summed = lambda half, begin, end: toep[:, s % NT, half, begin - Q:end - Q]

                def products(out_cols, stationary, table, begin, start, stop):
                    width = out_cols.shape[-1]
                    for n, (u, half) in enumerate(((0, 0), (0, 1), (1, 0))):
                        ins = M(out_cols, stationary[u], table(half, begin, begin + width),
                                start=start and n == 0, stop=stop and n == 2)
                    return ins

                for k in (half_blocks, 0, 1, 2, 3, 5, 6, 7):
                    u = (u_hi[:, s % 2, k, :], u_lo[:, s % 2, k, :])
                    r = k % half_blocks
                    at = 0 if k >= half_blocks else HALF
                    products(y[:, at:at + HALF - r * P], u, own, HALF + r * P, r == 0, r == half_blocks - 1)
                    if k < half_blocks // 2:
                        products(y[:, 0:Q], u, summed, Q + k * P, False, False)
                    elif k < half_blocks:
                        products(y[:, Q:2 * Q], u, summed, Q + k * P, False, False)
                pe.wait_ge(v_split, h + 1)
                for m in range(Q // P):
                    v = tuple(t[:, s % 2, m * P:(m + 1) * P] for t in (v_hi, v_lo))
                    ins = products(v_bank(s), v, own, Q + m * P, m == 0, m == Q // P - 1)
                ins.then_inc(conv_done, 1)

            def step2(i, first, last):
                for s in range(NX):
                    if s < NX - 1:
                        turn(i, s + 1, first)
                    elif not last:
                        turn(i + 1, 0, False)
                    conv(i, s, first)

            pe.wait_ge(x1_ready, PAIRS)
            turn(0, 0, True)
            step2(0, True, False)
            with pe.Fori(1, CSTEPS - 1) as i:
                step2(i, False, False)
            step2(CSTEPS - 1, False, True)


_INS = ['x', 'itok_B_0_7', 'itok_B_2182_4065', 'itok_B_78_3631', '_lenS', 'L0_cond_W_sess', 'L0_cond_b_sess',
        'L0_cond_W2', 'L0_cond_b2', 'L1_cond_log_dt', 'L1_cond_C', 'L1_cond_log_A_real', 'L1_cond_A_imag', 'L1_cond_D']
_OUTS = [((128, 64, 1024), 'float32')]


def kernel(**inputs):
    import numpy as _np
    import concourse.bacc as _bacc
    from concourse import mybir as _mybir
    from concourse.bass_utils import run_bass_kernel_spmd as _run

    nc = _bacc.Bacc("TRN2", target_bir_lowering=False, num_devices=1)
    arrays, args = {}, []
    for name in _INS:
        a = _np.ascontiguousarray(inputs[name])
        arrays[f"in_{name}_dram"] = a
        args.append(nc.dram_tensor(f"in_{name}_dram", a.shape, _mybir.dt.from_np(a.dtype), kind="ExternalInput").ap())
    for i, (shape, dtype) in enumerate(_OUTS):
        dt = _mybir.dt.from_np(_np.dtype(dtype))
        args.append(nc.dram_tensor(f"out_{i}_dram", shape, dt, kind="ExternalOutput").ap())
    build_cond_residual(nc, *args)
    r = _run(nc, [arrays], core_ids=[0])
    got = tuple(r.results[0][f"out_{i}_dram"] for i in range(len(_OUTS)))
    return got[0]
```
